# Optimizing a Trainium2 kernel written in Bass

```python
import numpy as np
import jax
import jax.numpy as jnp

def _softmax(x, axis=-1):
    return jax.nn.softmax(x, axis=axis)

def _gelu(x):
    return jax.nn.gelu(x, approximate=True)

def _silu(x):
    return jax.nn.silu(x)

def _sigmoid(x):
    return jax.nn.sigmoid(x)

def _layernorm(x, axis=-1, eps=1e-05):
    m = jnp.mean(x, axis=axis, keepdims=True)
    v = jnp.var(x, axis=axis, keepdims=True)
    return (x - m) / jnp.sqrt(v + eps)

def _scatter_add(tgt, idx, src, axis=0):
    return tgt.at[idx].add(src)

def _segment_sum(src, seg, n):
    return jax.ops.segment_sum(src, seg, n)
kernel_name = 'mk_adaln_d2_jaxref_r8_0b04e9'

def setup_inputs(seed: int=0):
    np.random.seed(seed)
    _w = jnp.asarray

    def _L0_attn_setup():
        import jax, jax.numpy as jnp
        import numpy as np
        import math
        D_MODEL = 256
        D_STATE = 64
        D_CONV = 4
        EXPAND = 2
        HEADDIM = 128
        NGROUPS = 1
        CHUNK = 32
        D_INNER = EXPAND * D_MODEL
        NHEADS = D_INNER // HEADDIM
        CONV_DIM = D_INNER + 2 * NGROUPS * D_STATE
        D_IN_PROJ = 2 * D_INNER + 2 * NGROUPS * D_STATE + NHEADS
        BATCH, SEQLEN = (2, 512)
        EPS = 1e-05

        def segsum(x):
            T = x.shape[-1]
            xx = jnp.broadcast_to(x[..., :, None], x.shape + (T,))
            mask_lo = jnp.tril(jnp.ones((T, T), dtype=bool), -1)
            xx = jnp.where(mask_lo, xx, 0.0)
            s = jnp.cumsum(xx, axis=-2)
            mask = jnp.tril(jnp.ones((T, T), dtype=bool), 0)
            return jnp.where(mask, s, -jnp.inf)

        def ssd(X, A, B, C, block_len):
            b, L, h, p = X.shape
            c = L // block_len
            X = X.reshape(b, c, block_len, h, p)
            A = A.reshape(b, c, block_len, h).transpose(0, 3, 1, 2)
            B = B.reshape(b, c, block_len, h, -1)
            C = C.reshape(b, c, block_len, h, -1)
            A_cumsum = jnp.cumsum(A, axis=-1)
            Lmat = jnp.exp(segsum(A))
            Y_diag = jnp.einsum('bclhn,bcshn,bhcls,bcshp->bclhp', C, B, Lmat, X)
            decay_states = jnp.exp(A_cumsum[:, :, :, -1:] - A_cumsum)
            states = jnp.einsum('bclhn,bhcl,bclhp->bchpn', B, decay_states, X)
            init = jnp.zeros_like(states[:, :1])
            states = jnp.concatenate([init, states], axis=1)
            decay_chunk = jnp.exp(segsum(jnp.pad(A_cumsum[:, :, :, -1], ((0, 0), (0, 0), (1, 0)))))
            new_states = jnp.einsum('bhzc,bchpn->bzhpn', decay_chunk, states)
            states, final_state = (new_states[:, :-1], new_states[:, -1])
            Y_off = jnp.einsum('bclhn,bchpn,bhcl->bclhp', C, states, jnp.exp(A_cumsum))
            Y = (Y_diag + Y_off).reshape(b, L, h, p)
            return (Y, final_state)

        def causal_dwconv(x, w, b):
            C, K = w.shape
            y = jax.lax.conv_general_dilated(x.transpose(0, 2, 1), w[:, None, :], (1,), [(K - 1, 0)], feature_group_count=C)
            return y.transpose(0, 2, 1) + b
        key = jax.random.key(seed)
        ks = jax.random.split(key, 8)
        u = jax.random.normal(ks[0], (BATCH, SEQLEN, D_MODEL), dtype=jnp.float32)
        W_in = jax.random.normal(ks[1], (D_MODEL, D_IN_PROJ), dtype=jnp.float32) / np.sqrt(D_MODEL)
        conv_w = jax.random.normal(ks[2], (CONV_DIM, D_CONV), dtype=jnp.float32) / np.sqrt(D_CONV)
        conv_b = jnp.zeros((CONV_DIM,), dtype=jnp.float32)
        dt_min, dt_max, dt_floor = (0.001, 0.1, 0.0001)
        dt = jnp.exp(jax.random.uniform(ks[3], (NHEADS,)) * (math.log(dt_max) - math.log(dt_min)) + math.log(dt_min))
        dt = jnp.clip(dt, dt_floor)
        dt_bias = dt + jnp.log(-jnp.expm1(-dt))
        A_log = jnp.log(jax.random.uniform(ks[4], (NHEADS,), minval=1.0, maxval=16.0))
        D = jnp.ones((NHEADS,), dtype=jnp.float32)
        norm_w = jnp.ones((D_INNER,), dtype=jnp.float32)
        W_out = jax.random.normal(ks[5], (D_INNER, D_MODEL), dtype=jnp.float32) / np.sqrt(D_INNER)
        return {'u': u, 'W_in': W_in, 'conv_w': conv_w, 'conv_b': conv_b, 'dt_bias': dt_bias, 'A_log': A_log, 'D': D, 'norm_w': norm_w, 'W_out': W_out}
    _L0_attn_in = _L0_attn_setup()

    def _L0_ffn_setup():
        import jax, jax.numpy as jnp
        import numpy as np
        B, S, D = (4, 256, 256)
        E = 8
        H = 352
        CAP_F = 1.0

        def _moe(x, Wg, W1, W3, W2, sw1, sw3, sw2):
            b, sl, d = x.shape
            T = b * sl
            C = int(CAP_F * T / E)
            xt = x.reshape(T, d)
            probs = jax.nn.softmax(xt @ Wg, axis=-1)
            eidx = jnp.argmax(probs, axis=-1)
            gate = jnp.take_along_axis(probs, eidx[:, None], 1)[:, 0]
            oh = jax.nn.one_hot(eidx, E, dtype=jnp.int32)
            pos = (jnp.cumsum(oh, axis=0) * oh).sum(-1) - 1
            keep = pos < C
            flat = jnp.where(keep, eidx * C + pos, E * C)
            xd = jnp.zeros((E * C, d), x.dtype).at[flat].set(xt, mode='drop')
            xd = xd.reshape(E, C, d)
            h = jax.nn.silu(jnp.einsum('ecd,edh->ech', xd, W1)) * jnp.einsum('ecd,edh->ech', xd, W3)
            oe = jnp.einsum('ech,ehd->ecd', h, W2).reshape(E * C, d)
            out = jnp.take(oe, jnp.minimum(flat, E * C - 1), axis=0)
            out = out * (gate * keep.astype(x.dtype))[:, None]
            shared = jax.nn.silu(xt @ sw1) * (xt @ sw3) @ sw2
            return (out + shared).reshape(b, sl, d)
        key = jax.random.key(seed)
        ks = jax.random.split(key, 8)
        s = lambda fan: 1.0 / np.sqrt(fan)
        return {'x': jax.random.normal(ks[0], (B, S, D), jnp.float32), 'Wg': jax.random.normal(ks[1], (D, E), jnp.float32) * s(D), 'W1': jax.random.normal(ks[2], (E, D, H), jnp.float32) * s(D), 'W3': jax.random.normal(ks[3], (E, D, H), jnp.float32) * s(D), 'W2': jax.random.normal(ks[4], (E, H, D), jnp.float32) * s(H), 'sw1': jax.random.normal(ks[5], (D, H), jnp.float32) * s(D), 'sw3': jax.random.normal(ks[6], (D, H), jnp.float32) * s(D), 'sw2': jax.random.normal(ks[7], (H, D), jnp.float32) * s(H)}
    _L0_ffn_in = _L0_ffn_setup()
    _L0_c = _w((lambda *s: np.random.randn(*s).astype(np.float32) * 0.05)(1, 256))
    _L0_wmod = _w((lambda *s: np.random.randn(*s).astype(np.float32) * 0.05)(256, 6 * 256) * 256 ** (-0.5))

    def _L1_attn_setup():
        import math
        import jax, jax.numpy as jnp
        import numpy as np
        H, KV, D = (16, 4, 128)
        HID = 256
        ROPE_BASE = 1000000.0
        EPS = 1e-06

        def _layernorm(x, w, b):
            mu = jnp.mean(x, axis=-1, keepdims=True)
            xc = x - mu
            var = jnp.mean(xc * xc, axis=-1, keepdims=True)
            return xc * jax.lax.rsqrt(var + EPS) * w + b

        def _rope(x, cos, sin):
            xr, xi = (x[..., 0::2], x[..., 1::2])
            c, s = (cos[None, None], sin[None, None])
            out = jnp.stack([xr * c - xi * s, xr * s + xi * c], axis=-1)
            return out.reshape(x.shape)
        key = jax.random.key(seed)
        ks = jax.random.split(key, 3)
        B, S = (2, 256)
        s = 0.02
        return {'x': jax.random.normal(ks[0], (B, S, HID), jnp.float32), 'w_qkv': jax.random.normal(ks[1], (2 * H * D + 2 * KV * D, HID), jnp.float32) * s, 'w_o': jax.random.normal(ks[2], (HID, H * D), jnp.float32) * s, 'q_norm_w': jnp.ones((D,), jnp.float32), 'q_norm_b': jnp.zeros((D,), jnp.float32), 'k_norm_w': jnp.ones((D,), jnp.float32), 'k_norm_b': jnp.zeros((D,), jnp.float32)}
    _L1_attn_in = _L1_attn_setup()

    def _L1_ffn_setup():
        import jax, jax.numpy as jnp
        import numpy as np

        def _sparsify_2to4(h):
            B, S, I = h.shape
            g = h.reshape(B, S, I // 4, 4)
            a = jnp.abs(g)
            _, idx = jax.lax.top_k(a, 2)
            pos = jnp.arange(4)
            mask = (pos == idx[..., 0:1]) | (pos == idx[..., 1:2])
            return (g * mask.astype(g.dtype)).reshape(B, S, I)
        key = jax.random.key(seed)
        k1, k2, k3, k4 = jax.random.split(key, 4)
        B, S, H, I = (4, 256, 256, 1024)
        x = jax.random.normal(k1, (B, S, H), dtype=jnp.float32)
        w_gate = jax.random.normal(k2, (H, I), dtype=jnp.float32) / np.sqrt(H)
        w_up = jax.random.normal(k3, (H, I), dtype=jnp.float32) / np.sqrt(H)
        w_down = jax.random.normal(k4, (I, H), dtype=jnp.float32) / np.sqrt(I)
        return {'x': x, 'w_gate': w_gate, 'w_up': w_up, 'w_down': w_down}
    _L1_ffn_in = _L1_ffn_setup()
    _L1_c = _w((lambda *s: np.random.randn(*s).astype(np.float32) * 0.05)(1, 256))
    _L1_wmod = _w((lambda *s: np.random.randn(*s).astype(np.float32) * 0.05)(256, 6 * 256) * 256 ** (-0.5))
    _d = {'L0_attn_u': _L0_attn_in['u'], 'L0_attn_W_in': _L0_attn_in['W_in'], 'L0_attn_conv_w': _L0_attn_in['conv_w'], 'L0_attn_conv_b': _L0_attn_in['conv_b'], 'L0_attn_dt_bias': _L0_attn_in['dt_bias'], 'L0_attn_A_log': _L0_attn_in['A_log'], 'L0_attn_D': _L0_attn_in['D'], 'L0_attn_norm_w': _L0_attn_in['norm_w'], 'L0_attn_W_out': _L0_attn_in['W_out'], 'L0_ffn_Wg': _L0_ffn_in['Wg'], 'L0_ffn_W1': _L0_ffn_in['W1'], 'L0_ffn_W3': _L0_ffn_in['W3'], 'L0_ffn_W2': _L0_ffn_in['W2'], 'L0_ffn_sw1': _L0_ffn_in['sw1'], 'L0_ffn_sw3': _L0_ffn_in['sw3'], 'L0_ffn_sw2': _L0_ffn_in['sw2'], 'L0_c': _L0_c, 'L0_wmod': _L0_wmod, 'L1_attn_w_qkv': _L1_attn_in['w_qkv'], 'L1_attn_w_o': _L1_attn_in['w_o'], 'L1_attn_q_norm_w': _L1_attn_in['q_norm_w'], 'L1_attn_q_norm_b': _L1_attn_in['q_norm_b'], 'L1_attn_k_norm_w': _L1_attn_in['k_norm_w'], 'L1_attn_k_norm_b': _L1_attn_in['k_norm_b'], 'L1_ffn_w_gate': _L1_ffn_in['w_gate'], 'L1_ffn_w_up': _L1_ffn_in['w_up'], 'L1_ffn_w_down': _L1_ffn_in['w_down'], 'L1_c': _L1_c, 'L1_wmod': _L1_wmod}
    _x0 = _d['L0_attn_u']
    _d['L0_attn_u'] = jax.random.normal(jax.random.fold_in(jax.random.key(seed), 1), (1, 1024, 256), dtype=_x0.dtype)
    del _x0
    return _d

def reference(L0_attn_u, L0_attn_W_in, L0_attn_conv_w, L0_attn_conv_b, L0_attn_dt_bias, L0_attn_A_log, L0_attn_D, L0_attn_norm_w, L0_attn_W_out, L0_ffn_Wg, L0_ffn_W1, L0_ffn_W3, L0_ffn_W2, L0_ffn_sw1, L0_ffn_sw3, L0_ffn_sw2, L0_c, L0_wmod, L1_attn_w_qkv, L1_attn_w_o, L1_attn_q_norm_w, L1_attn_q_norm_b, L1_attn_k_norm_w, L1_attn_k_norm_b, L1_ffn_w_gate, L1_ffn_w_up, L1_ffn_w_down, L1_c, L1_wmod):

    def _L0_attn_ref(u, W_in, conv_w, conv_b, dt_bias, A_log, D, norm_w, W_out):
        import jax, jax.numpy as jnp
        import numpy as np
        import math
        D_MODEL = 256
        D_STATE = 64
        D_CONV = 4
        EXPAND = 2
        HEADDIM = 128
        NGROUPS = 1
        CHUNK = 32
        D_INNER = EXPAND * D_MODEL
        NHEADS = D_INNER // HEADDIM
        CONV_DIM = D_INNER + 2 * NGROUPS * D_STATE
        D_IN_PROJ = 2 * D_INNER + 2 * NGROUPS * D_STATE + NHEADS
        BATCH, SEQLEN = (2, 512)
        EPS = 1e-05

        def segsum(x):
            T = x.shape[-1]
            xx = jnp.broadcast_to(x[..., :, None], x.shape + (T,))
            mask_lo = jnp.tril(jnp.ones((T, T), dtype=bool), -1)
            xx = jnp.where(mask_lo, xx, 0.0)
            s = jnp.cumsum(xx, axis=-2)
            mask = jnp.tril(jnp.ones((T, T), dtype=bool), 0)
            return jnp.where(mask, s, -jnp.inf)

        def ssd(X, A, B, C, block_len):
            b, L, h, p = X.shape
            c = L // block_len
            X = X.reshape(b, c, block_len, h, p)
            A = A.reshape(b, c, block_len, h).transpose(0, 3, 1, 2)
            B = B.reshape(b, c, block_len, h, -1)
            C = C.reshape(b, c, block_len, h, -1)
            A_cumsum = jnp.cumsum(A, axis=-1)
            Lmat = jnp.exp(segsum(A))
            Y_diag = jnp.einsum('bclhn,bcshn,bhcls,bcshp->bclhp', C, B, Lmat, X)
            decay_states = jnp.exp(A_cumsum[:, :, :, -1:] - A_cumsum)
            states = jnp.einsum('bclhn,bhcl,bclhp->bchpn', B, decay_states, X)
            init = jnp.zeros_like(states[:, :1])
            states = jnp.concatenate([init, states], axis=1)
            decay_chunk = jnp.exp(segsum(jnp.pad(A_cumsum[:, :, :, -1], ((0, 0), (0, 0), (1, 0)))))
            new_states = jnp.einsum('bhzc,bchpn->bzhpn', decay_chunk, states)
            states, final_state = (new_states[:, :-1], new_states[:, -1])
            Y_off = jnp.einsum('bclhn,bchpn,bhcl->bclhp', C, states, jnp.exp(A_cumsum))
            Y = (Y_diag + Y_off).reshape(b, L, h, p)
            return (Y, final_state)

        def causal_dwconv(x, w, b):
            C, K = w.shape
            y = jax.lax.conv_general_dilated(x.transpose(0, 2, 1), w[:, None, :], (1,), [(K - 1, 0)], feature_group_count=C)
            return y.transpose(0, 2, 1) + b
        batch, seqlen, _ = u.shape
        zxbcdt = u @ W_in
        z, xBC, dt = jnp.split(zxbcdt, [D_INNER, D_INNER + CONV_DIM], axis=-1)
        dt = jax.nn.softplus(dt + dt_bias)
        xBC = jax.nn.silu(causal_dwconv(xBC, conv_w, conv_b))
        x, B, C = jnp.split(xBC, [D_INNER, D_INNER + NGROUPS * D_STATE], axis=-1)
        x = x.reshape(batch, seqlen, NHEADS, HEADDIM)
        B = jnp.broadcast_to(B.reshape(batch, seqlen, NGROUPS, D_STATE), (batch, seqlen, NHEADS, D_STATE))
        C = jnp.broadcast_to(C.reshape(batch, seqlen, NGROUPS, D_STATE), (batch, seqlen, NHEADS, D_STATE))
        A = -jnp.exp(A_log)
        x_scaled = x * dt[..., None]
        A_dt = A * dt
        y, _final = ssd(x_scaled, A_dt, B, C, CHUNK)
        y = y.reshape(batch, seqlen, D_INNER)
        x_flat = x.reshape(batch, seqlen, D_INNER)
        D_full = jnp.repeat(D, HEADDIM)
        y = y + x_flat * D_full
        yg = y * jax.nn.silu(z)
        var = jnp.mean(yg * yg, axis=-1, keepdims=True)
        y = yg * jax.lax.rsqrt(var + EPS) * norm_w
        return y @ W_out

    def _L0_ffn_ref(x, Wg, W1, W3, W2, sw1, sw3, sw2):
        import jax, jax.numpy as jnp
        import numpy as np
        B, S, D = (4, 256, 256)
        E = 8
        H = 352
        CAP_F = 1.0

        def _moe(x, Wg, W1, W3, W2, sw1, sw3, sw2):
            b, sl, d = x.shape
            T = b * sl
            C = int(CAP_F * T / E)
            xt = x.reshape(T, d)
            probs = jax.nn.softmax(xt @ Wg, axis=-1)
            eidx = jnp.argmax(probs, axis=-1)
            gate = jnp.take_along_axis(probs, eidx[:, None], 1)[:, 0]
            oh = jax.nn.one_hot(eidx, E, dtype=jnp.int32)
            pos = (jnp.cumsum(oh, axis=0) * oh).sum(-1) - 1
            keep = pos < C
            flat = jnp.where(keep, eidx * C + pos, E * C)
            xd = jnp.zeros((E * C, d), x.dtype).at[flat].set(xt, mode='drop')
            xd = xd.reshape(E, C, d)
            h = jax.nn.silu(jnp.einsum('ecd,edh->ech', xd, W1)) * jnp.einsum('ecd,edh->ech', xd, W3)
            oe = jnp.einsum('ech,ehd->ecd', h, W2).reshape(E * C, d)
            out = jnp.take(oe, jnp.minimum(flat, E * C - 1), axis=0)
            out = out * (gate * keep.astype(x.dtype))[:, None]
            shared = jax.nn.silu(xt @ sw1) * (xt @ sw3) @ sw2
            return (out + shared).reshape(b, sl, d)
        return _moe(x, Wg, W1, W3, W2, sw1, sw3, sw2)

    def _L1_attn_ref(x, w_qkv, w_o, q_norm_w, q_norm_b, k_norm_w, k_norm_b):
        import math
        import jax, jax.numpy as jnp
        import numpy as np
        H, KV, D = (16, 4, 128)
        HID = 256
        ROPE_BASE = 1000000.0
        EPS = 1e-06

        def _layernorm(x, w, b):
            mu = jnp.mean(x, axis=-1, keepdims=True)
            xc = x - mu
            var = jnp.mean(xc * xc, axis=-1, keepdims=True)
            return xc * jax.lax.rsqrt(var + EPS) * w + b

        def _rope(x, cos, sin):
            xr, xi = (x[..., 0::2], x[..., 1::2])
            c, s = (cos[None, None], sin[None, None])
            out = jnp.stack([xr * c - xi * s, xr * s + xi * c], axis=-1)
            return out.reshape(x.shape)
        B, S, _ = x.shape
        qkv = x @ w_qkv.T
        qg, k, v = jnp.split(qkv, [2 * H * D, 2 * H * D + KV * D], axis=-1)
        q, gate = jnp.split(qg, 2, axis=-1)
        q = q.reshape(B, S, H, D).transpose(0, 2, 1, 3)
        k = k.reshape(B, S, KV, D).transpose(0, 2, 1, 3)
        v = v.reshape(B, S, KV, D).transpose(0, 2, 1, 3)
        q = _layernorm(q, q_norm_w, q_norm_b)
        k = _layernorm(k, k_norm_w, k_norm_b)
        inv = 1.0 / ROPE_BASE ** (jnp.arange(0, D, 2, dtype=jnp.float32) / D)
        freqs = jnp.outer(jnp.arange(S, dtype=jnp.float32), inv)
        cos, sin = (jnp.cos(freqs), jnp.sin(freqs))
        q = _rope(q, cos, sin)
        k = _rope(k, cos, sin)
        rep = H // KV
        k = jnp.repeat(k, rep, axis=1)
        v = jnp.repeat(v, rep, axis=1)
        scores = jnp.einsum('bhqd,bhkd->bhqk', q, k) / math.sqrt(D)
        causal = jnp.tril(jnp.ones((S, S), bool))
        scores = jnp.where(causal[None, None], scores, -jnp.inf)
        attn = jax.nn.softmax(scores, axis=-1)
        out = jnp.einsum('bhqk,bhkd->bhqd', attn, v)
        out = out.transpose(0, 2, 1, 3).reshape(B, S, H * D)
        out = out * jax.nn.sigmoid(gate)
        return out @ w_o.T

    def _L1_ffn_ref(x, w_gate, w_up, w_down):
        import jax, jax.numpy as jnp
        import numpy as np

        def _sparsify_2to4(h):
            B, S, I = h.shape
            g = h.reshape(B, S, I // 4, 4)
            a = jnp.abs(g)
            _, idx = jax.lax.top_k(a, 2)
            pos = jnp.arange(4)
            mask = (pos == idx[..., 0:1]) | (pos == idx[..., 1:2])
            return (g * mask.astype(g.dtype)).reshape(B, S, I)
        h = jax.nn.silu(jnp.einsum('bsh,hi->bsi', x, w_gate)) * jnp.einsum('bsh,hi->bsi', x, w_up)
        h_sparse = _sparsify_2to4(h)
        return jnp.einsum('bsi,ih->bsh', h_sparse, w_down)
    x = L0_attn_u
    mod = (_silu(L0_c) @ L0_wmod).reshape(L0_c.shape[0], 6, 1, -1)
    sa, ca, ga, sb, cb, gb = (mod[:, 0], mod[:, 1], mod[:, 2], mod[:, 3], mod[:, 4], mod[:, 5])
    ga = (2 * (ga >= 0) - 1) * jnp.maximum(jnp.abs(ga), 0.25)
    gb = (2 * (gb >= 0) - 1) * jnp.maximum(jnp.abs(gb), 0.25)
    h = _layernorm(x, axis=-1) * (1 + ca) + sa
    x = x + ga * _L0_attn_ref(h, L0_attn_W_in, L0_attn_conv_w, L0_attn_conv_b, L0_attn_dt_bias, L0_attn_A_log, L0_attn_D, L0_attn_norm_w, L0_attn_W_out)
    h = _layernorm(x, axis=-1) * (1 + cb) + sb
    x = x + gb * _L0_ffn_ref(h, L0_ffn_Wg, L0_ffn_W1, L0_ffn_W3, L0_ffn_W2, L0_ffn_sw1, L0_ffn_sw3, L0_ffn_sw2)
    mod = (_silu(L1_c) @ L1_wmod).reshape(L1_c.shape[0], 6, 1, -1)
    sa, ca, ga, sb, cb, gb = (mod[:, 0], mod[:, 1], mod[:, 2], mod[:, 3], mod[:, 4], mod[:, 5])
    ga = (2 * (ga >= 0) - 1) * jnp.maximum(jnp.abs(ga), 0.25)
    gb = (2 * (gb >= 0) - 1) * jnp.maximum(jnp.abs(gb), 0.25)
    h = _layernorm(x, axis=-1) * (1 + ca) + sa
    x = x + ga * _L1_attn_ref(h, L1_attn_w_qkv, L1_attn_w_o, L1_attn_q_norm_w, L1_attn_q_norm_b, L1_attn_k_norm_w, L1_attn_k_norm_b)
    h = _layernorm(x, axis=-1) * (1 + cb) + sb
    x = x + gb * _L1_ffn_ref(h, L1_ffn_w_gate, L1_ffn_w_up, L1_ffn_w_down)
    return x

_drawn_inputs = setup_inputs


def setup_inputs(seed=0):
    import zlib

    import numpy as np

    out = dict(_drawn_inputs(seed))
    spreads = {'L0_attn_conv_b': (0.0, 0.1),
     'L0_attn_D': (1.0, 0.6),
     'L0_attn_norm_w': (1.0, 0.2),
     'L1_attn_q_norm_w': (1.0, 0.6),
     'L1_attn_q_norm_b': (0.0, 0.8),
     'L1_attn_k_norm_w': (1.0, 0.6),
     'L1_attn_k_norm_b': (0.0, 0.8)}
    factors = {'L0_attn_A_log': 3.221, 'L1_attn_w_qkv': 8.0, 'L1_attn_w_o': 8.0}
    for name, (base, spread) in spreads.items():
        noise = np.random.default_rng([zlib.crc32(name.encode()), seed]).standard_normal(out[name].shape)
        drawn = base * np.exp(spread * noise) if base else spread * noise
        out[name] = jnp.asarray(drawn.astype(out[name].dtype))
    for name, factor in factors.items():
        out[name] = (out[name] * factor).astype(out[name].dtype)
    return out
```

```python
from contextlib import ExitStack

import concourse.bass as bass
import numpy as np
from concourse import mybir

ALU = mybir.AluOpType
ACT = mybir.ActivationFunctionType
F32 = mybir.dt.float32
BF16 = mybir.dt.bfloat16
U32 = mybir.dt.uint32
AX_X = mybir.AxisListType.X

P = 128
T = 1024
NT = T // P
D = 256
KD = D // P
DI = 512
NH = 4
NS = 64
E = 8
CAP = T // E
H = 352
KH = 3
HP = KH * P
HQ, HKV, DH = 16, 4, 128
REP = HQ // HKV
FF = 1024
MASKED = -1e30
NEVER = 4096.0


class PsumPlan:

    def __init__(self):
        self.turn = {}
        self.used = {}

    def add(self, job, slot):
        assert job not in self.turn, job
        self.turn[job] = (slot, self.used.get(slot, 0))
        self.used[slot] = self.used.get(slot, 0) + 1


def layer0_jobs():
    jobs = [("modcol",), ("modrow", 0), ("modrow", 1)]
    jobs += [("hT", "mix", g) for g in range(NT // 2)]
    jobs += [("dt",)]
    for n in range(2):
        jobs += [("xbc", n, m) for m in range(5)]
        jobs += [("z", i) for i in range(4 * n, 4 * n + 4)]
    front = lambda c: [("xtok", c), ("misc", c), ("seg", c)]
    jobs += front(0)
    for c in range(NT):
        jobs += [("yoff", c), ("ydiag", c), ("state", c)]
        jobs += front(c + 1) if c + 1 < NT else []
        jobs += [("ygT", c), ("mixout", c)]
    jobs += [("hT", "moe", g) for g in range(NT // 2)]
    jobs += [("logits",), ("rank",)]
    for n in range(2):
        for m in range(KH):
            jobs += [("sh1", n, m), ("sh3", n, m)]
        jobs += [("shout", i) for i in range(4 * n, 4 * n + 4)]
    jobs += [("xdT", g) for g in range(4)]
    jobs += [("e1", 0), ("e3", 0)]
    for e in range(E):
        jobs += [("e1", e + 1), ("e3", e + 1)] if e + 1 < E else []
        jobs += [("eout", e)]
    return jobs


BESIDE = {
    0: [("ln3", 1), ("oT", -1, 3)],
    1: [("gate", 0, 1), ("h3T", 1), ("wo", -1)],
    2: [("proj", 1, "k"), ("eT", 1), ("ln4", -1)],
    3: [("proj", 1, "v"), ("rope", 1, "k"), ("h4T", -1)],
    4: [("proj", 1, 0), ("qkT", 1, "k"), ("oT", 0, 0)],
    5: [("gate", 0, 2), ("rope", 1, 0), ("gu", -1, 0)],
    6: [("proj", 1, 1), ("qkT", 1, 0), ("gu", -1, 1)],
    7: [("rope", 1, 1), ("gu", -1, 2)],
    8: [("gu", -1, 3), ("qkT", 1, 1), ("oT", 0, 1)],
    9: [("proj", 1, 2), ("sparse", -1)],
    10: [("gate", 0, 3), ("rope", 1, 2)],
    11: [("hsT", -1, 0), ("hsT", -1, 1), ("qkT", 1, 2)],
    12: [("proj", 1, 3), ("oT", 0, 2)],
    13: [("rope", 1, 3), ("down", -1)],
    14: [("gate", 1, 0)],
    15: [("qkT", 1, 3)],
}


def layer1_steps():
    first = [("ln3",), ("h3T",), ("proj", "k"), ("proj", 0), ("proj", "v"), ("eT",), ("rope", "k"),
             ("proj", 1), ("rope", 0), ("qkT", "k"), ("proj", 2), ("rope", 1), ("qkT", 0),
             ("proj", 3), ("rope", 2), ("qkT", 1), ("gate", 0), ("rope", 3), ("qkT", 2), ("qkT", 3)]
    last = [("oT", 3), ("wo",), ("ln4",), ("h4T",), ("gu", 0), ("gu", 1), ("gu", 2), ("gu", 3),
            ("sparse",), ("hsT", 0), ("hsT", 1), ("down",)]
    steps = [(None, [(kind, 0, *rest)]) for kind, *rest in first]
    for i in range(NT):
        for h in range(HQ):
            steps.append(((i, h), [(kind, i + di, *rest) for kind, di, *rest in BESIDE[h]
                                   if 0 <= i + di < NT]))
    return steps + [(None, [(kind, NT - 1, *rest)]) for kind, *rest in last]


AHEAD = 2


def after(att):
    i, h = att
    n = i * HQ + h + AHEAD
    return (n // HQ, n % HQ) if n < NT * HQ else None


def groups(i):
    return [range(j, min(j + 4, i + 1)) for j in range(0, i + 1, 4)]


PSUM_OF = {"proj": "M", "gate": "M", "wo": "M", "gu": "M", "down": "M",
           "h3T": "T", "h4T": "T", "eT": "T", "qkT": "T", "oT": "T", "hsT": "T"}


def layer1_jobs(steps):
    jobs = []
    turns = 0
    for att, beside in steps:
        if att == (0, 0):
            jobs += [(("S", 0, h), f"S{h % 2}") for h in range(AHEAD)]
        if att:
            for g in range(len(groups(att[0]))):
                jobs.append((("PT", *att, g), f"T{turns % 2}"))
                turns += 1
        if att and after(att):
            i, h = after(att)
            jobs.append((("S", i, h), f"S{h % 2}"))
        for work in beside:
            if work[0] in PSUM_OF:
                slot = PSUM_OF[work[0]]
                if slot == "T":
                    slot = f"T{turns % 2}"
                    turns += 1
                elif att is None:
                    slot = ("M", "O", "S0", "S1")[len(jobs) % 4]
                jobs.append((work, slot))
        if att:
            jobs.append((("O", *att), "O"))
    return jobs


def build(nc, consts_d, tables_d, vectors_d, x_d, W_in_d, W_out_d, Wg_d, W1_d, W3_d, W2_d, sw1_d,
          sw3_d, sw2_d, wmod0_d, wmod1_d, wqkv_d, wo_d, wgate_d, wup_d, wdown_d, out_d):
    xd_d = nc.dram_tensor("expert_rows", [E * CAP, D], F32, kind="Internal").ap()
    oe_d = nc.dram_tensor("expert_outputs", [E * CAP, D], F32, kind="Internal").ap()
    ctx = ExitStack()
    with ctx:
        def sb(name, words, dt=F32, parts=P):
            return ctx.enter_context(nc.sbuf_tensor(name, [parts, words], dt))

        def sem(name):
            return ctx.enter_context(nc.semaphore(name))

        consts = sb("consts", 512)
        ident, tri, stril = (consts[:, k * P:(k + 1) * P] for k in range(3))
        rank_weight, expert_base = consts[:, 384:448], consts[:, 448:512]
        rope_cos_sin = sb("rope_cos_sin", 2 * NT * 64)
        rope_cs = rope_cos_sin[:, :].rearrange("p (a i d) -> p a i d", a=2, i=NT)
        x = sb("x", NT * D)[:, :].rearrange("p (i d) -> p i d", i=NT)
        vectors = sb("vectors", 560)
        c_cols = vectors[:, 0:4]
        dt_bias, a_log, d_skip = vectors[:, 4:8], vectors[:, 8:12], vectors[:, 12:16]
        norm_w = vectors[:, 16:20]
        conv_w = vectors[:, 20:40].rearrange("p (m j) -> p m j", m=5)
        conv_b = vectors[:, 40:45]
        ln_w = vectors[:, 48:304].rearrange("p (ri qk d) -> p ri qk d", ri=2, qk=2)
        ln_b = vectors[:, 304:560].rearrange("p (ri qk d) -> p ri qk d", ri=2, qk=2)
        ones = sb("ones", P)
        ident_h = sb("ident_h", P, BF16)
        mask_h = sb("mask_h", P, BF16)
        mod_col = sb("mod_col", 16)
        g_row = sb("g_row", 2 * 512)[:, :].rearrange("p (l n) -> p l n", l=2)
        ln_st = sb("ln_st", 4 * 6)[:, :].rearrange("p (s n) -> p s n", s=4)
        ln_mv = sb("ln_mv", 4 * 2)[:, :].rearrange("p (s n) -> p s n", s=4)
        ln_rstd = sb("ln_rstd", 4)
        ln_t = sb("ln_t", 4)
        half_neg = sb("half_neg", 4)
        xtmp = sb("xtmp", D)
        route = sb("route", 5 * 64)[:, :].rearrange("p (s n) -> p s n", s=5)
        rt8 = sb("rt8", 9 * 8)[:, :].rearrange("p (s n) -> p s n", s=9)
        slot_u = sb("slot_u", 2 * 8, U32)[:, :].rearrange("p (s n) -> p s n", s=2)
        dtb = sb("dtb", 12 * 32)[:, :].rearrange("p (s n) -> p s n", s=12)
        small = sb("small", 64)
        a_dt = lambda c: dtb[:, 10, c * NH:(c + 1) * NH]
        dt_as_relu = dtb[:, 11, :]

        words = (nc.sbuf_usable_end - nc.sbuf_base) // 4 - 40
        arena = sb("arena", words)

        class Region:
            def __init__(self, at, end):
                self.at, self.end = at, end

            def take(self, n):
                a = arena[:, self.at:self.at + n]
                self.at += n
                assert self.at <= self.end, (self.at, self.end)
                return a

        TAIL = 2 * E * KD * HP + 3 * KH * D
        moe_at = words - TAIL
        r = Region(moe_at, words)
        W1 = r.take(E * KD * HP).rearrange("p (e k h) -> p e k h", e=E, k=KD)
        W3 = r.take(E * KD * HP).rearrange("p (e k h) -> p e k h", e=E, k=KD)
        sw1 = r.take(KD * HP).rearrange("p (k h) -> p k h", k=KD)
        sw3 = r.take(KD * HP).rearrange("p (k h) -> p k h", k=KD)
        sw2 = r.take(KH * D).rearrange("p (k n) -> p k n", k=KH)
        r = Region(0, moe_at)
        xn = r.take(NT * D).rearrange("p (i d) -> p i d", i=NT)
        hT = r.take(KD * T).rearrange("p (k t) -> p k t", k=KD)
        Wg = r.take(KD * E).rearrange("p (k e) -> p k e", k=KD)
        moe_acts = r.at
        W_in = r.take(KD * 1156).rearrange("p (k n) -> p k n", k=KD)
        W_out = r.take(4 * D).rearrange("p (k n) -> p k n", k=4)
        xc = r.take(5 * (T + 3)).rearrange("p (m t) -> p m t", m=5)
        xT = r.take(5 * T).rearrange("p (m t) -> p m t", m=5)
        BT = xT[:, 4, :]
        CT = r.take(T)
        wmod_at = r.at
        zs = r.take(NT * DI).rearrange("p (i n) -> p i n", i=NT)
        two = lambda n: r.take(2 * n).rearrange("p (b n) -> p b n", b=2)
        x_sb = r.take(DI).rearrange("p (h d) -> p h d", h=NH)
        Xdt, xD, M1, MT, Xs, S = (two(DI).rearrange("p b (h d) -> p b h d", h=NH) for _ in range(6))
        Lm = r.take(DI).rearrange("p (h d) -> p h d", h=NH)
        Gm = r.take(P)
        y1, yg, ygT = (r.take(DI).rearrange("p (h d) -> p h d", h=NH) for _ in range(3))
        B_tok = two(NS)
        es = two(8)
        sq_out = xc[:, 0, 0:DI]
        zeros = ygT[:, 0:2, :].rearrange("p a b -> p (a b)")
        r = Region(wmod_at, moe_at)
        wmod = r.take(2 * KD * 1536).rearrange("p (l k n) -> p l k n", l=2, k=KD)
        sc_b = r.take(4 * P).rearrange("p (s n) -> p s n", s=4)
        g_abs = r.take(512)
        r = Region(moe_acts, moe_at)
        wqkv = r.take(KD * 5120).rearrange("p (k n) -> p k n", k=KD)
        l1_acts = r.at
        W2 = r.take(E * KH * D).rearrange("p (e k n) -> p e k n", e=E, k=KH)
        hs = r.take(KH * T).rearrange("p (k t) -> p k t", k=KH)
        s1 = r.take(2 * 512).rearrange("p (b n) -> p b n", b=2)
        xd = r.take(E * D).rearrange("p (e d) -> p e d", e=E)
        og = xd
        xdT = r.take(KD * E * P).rearrange("p (k e s) -> p k e s", k=KD, e=E)
        se = r.take(2 * HP).rearrange("p (b n) -> p b n", b=2)
        he = r.take(2 * HP).rearrange("p (b n) -> p b n", b=2)
        oe = hs.rearrange("p k t -> p (k t)")[:, 0:E * D].rearrange("p (e d) -> p e d", e=E)
        r = Region(moe_at, words)
        wo = r.take(HQ * D).rearrange("p (h n) -> p h n", h=HQ)
        wgate = r.take(KD * FF).rearrange("p (k n) -> p k n", k=KD)
        wup = r.take(KD * FF).rearrange("p (k n) -> p k n", k=KD)
        wdown = r.take(FF // P * D).rearrange("p (k n) -> p k n", k=FF // P)
        sg = r.take(FF)
        tb = r.take(FF)
        hsT = r.take(FF).rearrange("p (k t) -> p k t", k=FF // P)
        spt_h = hsT[:, 0:4, :].rearrange("p k t -> p (k t)").bitcast(BF16).rearrange("p (n g) -> p n g", n=4)
        h4T = r.take(D).rearrange("p (k t) -> p k t", k=KD)
        cmp_h = r.take(6 * P).bitcast(BF16).rearrange("p (c g) -> p c g", c=6)
        r = Region(l1_acts, moe_at)
        kT = r.take(HKV * T).rearrange("p (h t) -> p h t", h=HKV)
        v = r.take(NT * HKV * DH).rearrange("p (i n) -> p i n", i=NT)
        qT = r.take(HQ * P).rearrange("p (h t) -> p h t", h=HQ)
        pr = two(T)
        oT = r.take(HQ * P).rearrange("p (h t) -> p h t", h=HQ)
        PT = two(512)
        gate = two(512)
        raw, roped = (r.take(512).rearrange("p (h d) -> p h d", h=4) for _ in range(2))
        r = Region(0, moe_acts)
        xn1 = two(D)
        raws = [oT[:, 4 * n:4 * n + 4, :] for n in range(4)]
        ropeds = [pr[:, n // 2, n % 2 * 512:(n % 2 + 1) * 512].rearrange("p (h d) -> p h d", h=4) for n in range(4)]
        raw_of = lambda r_no: raws[r_no] if r_no < 4 else raw
        roped_of = lambda r_no: ropeds[r_no] if r_no < 4 else roped
        h3T = two(D).rearrange("p b (k t) -> p b k t", k=KD)
        osb = r.take(512)
        rt = r.take(4 * 128).rearrange("p (s qk d) -> p s qk d", s=4, qk=2)
        rope_E = r.take(256).rearrange("p (qk d) -> p qk d", qk=2)
        eT = r.take(256).rearrange("p (qk t) -> p qk t", qk=2)
        rtmp = r.take(256)
        t_r = r.take(512).rearrange("p (s h d) -> p s h d", s=2, h=4)
        t_i = r.take(512).rearrange("p (s h d) -> p s h d", s=2, h=4)
        q_st = r.take(2 * 4 * 6).rearrange("p (b h n) -> p b h n", b=2, h=4)
        q_mv = r.take(2 * 4 * 2).rearrange("p (b h n) -> p b h n", b=2, h=4)
        q_rs = two(4)
        q_tt = two(4)
        nmax, rsum, rinv = r.take(4), r.take(4), r.take(4)

        psum = ctx.enter_context(nc.psum_tensor("psum", [P, 8, 512], F32))

        steps = layer1_steps()
        plan = PsumPlan()
        for n, job in enumerate(layer0_jobs()):
            plan.add(job, n % 8)
        for job, slot in layer1_jobs(steps):
            plan.add(job, slot)
        BANK_OF = {"S0": 0, "S1": 2, "T0": 4, "T1": 5, "O": 6, "M": 7}
        filled = {s: sem(f"filled_{s}") for s in plan.used}
        drained = {s: sem(f"drained_{s}") for s in plan.used}

        def bank(job):
            slot = plan.turn[job][0]
            b = BANK_OF.get(slot, slot)
            if job[0] == "S":
                return psum[:, b:b + 2, :].rearrange("p b n -> p (b n)")
            return psum[:, b, :]

        def landed(eng, job):
            slot, n = plan.turn[job]
            eng.wait_ge(filled[slot], n + 1)

        def taken(eng, job):
            slot, n = plan.turn[job]
            eng.wait_ge(drained[slot], n + 1)

        def is_drained(job):
            return drained[plan.turn[job][0]]

        def is_filled(job):
            return filled[plan.turn[job][0]]

        ln_order = [("mix", i) for i in range(NT)] + [("moe", i) for i in range(NT)]
        for _, beside in steps:
            ln_order += [(w[0], w[1]) for w in beside if w[0] in ("ln3", "ln4")]
        ln_no = {key: n for n, key in enumerate(ln_order)}
        sparse_no = lambda i: i + 1
        rope_no = {}
        for i in range(NT):
            for c in ("k", 0, 1, 2, 3):
                rope_no[i, c] = len(rope_no)
        pt_no = {}
        for i in range(NT):
            for h in range(HQ):
                for g in range(len(groups(i))):
                    pt_no[i, h, g] = len(pt_no)
        pt_key = {n: key for key, n in pt_no.items()}

        names = ["consts", "tables", "vectors", "x", "W_in", "W_out", "Wg", "W1", "W3", "W2",
                 "sw", "wmod", "wqkv", "wo", "wffn", "xd_rows"]
        loaded = {n: sem(f"loaded_{n}") for n in names}
        zeroed = sem("zeroed")
        scattered = sem("scattered")
        oe_stored = sem("oe_stored")
        gathered = sem("gathered")
        stored = sem("stored")
        pool_init = sem("pool_init")
        dve_init = sem("dve_init")
        sc_ready = sem("sc_ready")
        scb_ready = sem("scb_ready")
        g_ready = sem("g_ready")
        dve = sem("dve")
        act = sem("act")
        pool = sem("pool")
        ln_stats, ln_scaled, ln_done = sem("ln_stats"), sem("ln_scaled"), sem("ln_done")
        conv_in, conv_done, conv_silu = sem("conv_in"), sem("conv_done"), sem("conv_silu")
        dt_abs, dt_exp, a_exp, dt_ready = sem("dt_abs"), sem("dt_exp"), sem("a_exp"), sem("dt_ready")
        m1_ready, misc_act, xdt_ready = sem("m1_ready"), sem("misc_act"), sem("xdt_ready")
        mt_ready, xs_ready, y_ready = sem("mt_ready"), sem("xs_ready"), sem("y_ready")
        yg_ready, yg_sq, yg_rstd = sem("yg_ready"), sem("yg_sq"), sem("yg_rstd")
        x_mixed = sem("x_mixed")
        moe_free = sem("moe_free")
        route_d, route_e, oh_ready, route_done = (sem("route_d"), sem("route_e"), sem("oh_ready"),
                                                  sem("route_done"))
        s1_ready, se_ready = sem("s1_ready"), sem("se_ready")
        x_shared, x_moe = sem("x_shared"), sem("x_moe")
        tab_ready, q_stats, q_rstd, q_norm = (sem("tab_ready"), sem("q_stats"), sem("q_rstd"),
                                              sem("q_norm"))
        rope_r, rope_i = sem("rope_r"), sem("rope_i")
        maxed = sem("maxed")
        gate_tanh, gate_ready = sem("gate_tanh"), sem("gate_ready")
        x_att, x_out = sem("x_att"), sem("x_out")
        gu_tanh, sparse_ready = sem("gu_tanh"), sem("sparse_ready")

        block = ctx.enter_context(nc.Block())

        @block.sync
        def _(sp):
            sp.dma_start(consts[:, :], consts_d).then_inc(loaded["consts"], 16)
            sp.dma_start(vectors[:, :], vectors_d).then_inc(loaded["vectors"], 16)
            for l, w in enumerate((wmod0_d, wmod1_d)):
                sp.dma_start(wmod[:, l], w.rearrange("(k p) n -> p k n", p=P)).then_inc(loaded["wmod"], 16)
            sp.dma_start(x, x_d[0].rearrange("(i p) d -> p i d", p=P)).then_inc(loaded["x"], 16)
            sp.dma_start(W_in, W_in_d.rearrange("(k p) n -> p k n", p=P)).then_inc(loaded["W_in"], 16)
            sp.dma_start(W_out, W_out_d.rearrange("(k p) n -> p k n", p=P)).then_inc(loaded["W_out"], 16)
            sp.dma_start(Wg, Wg_d.rearrange("(k p) n -> p k n", p=P)).then_inc(loaded["Wg"], 16)
            sp.wait_ge(pool_init, 1)
            for w, w_d in ((sw1, sw1_d), (sw3, sw3_d)):
                sp.dma_start(w[:, :, 0:H], w_d.rearrange("(k p) h -> p k h", p=P)).then_inc(loaded["sw"], 16)
            sp.dma_start(sw2[:, 0:2, :], sw2_d[0:2 * P].rearrange("(k p) n -> p k n", p=P)).then_inc(loaded["sw"], 16)
            sp.dma_start(sw2[0:H - 2 * P, 2, :], sw2_d[2 * P:H]).then_inc(loaded["sw"], 16)
            sp.wait_ge(dve_init, 1)
            sp.dma_start(xd_d.rearrange("(e s) d -> s e d", e=E),
                         zeros.unsqueeze(1).to_broadcast([P, E, D])).then_inc(zeroed, 16)
            for e in range(E):
                sp.dma_start(W1[:, e, :, 0:H], W1_d[e].rearrange("(k p) h -> p k h", p=P)).then_inc(loaded["W1"], 16)
                sp.dma_start(W3[:, e, :, 0:H], W3_d[e].rearrange("(k p) h -> p k h", p=P)).then_inc(loaded["W3"], 16)
            sp.dma_start(rope_cos_sin[:, :], tables_d).then_inc(loaded["tables"], 16)
            sp.wait_ge(x_mixed, NT)
            sp.wait_ge(moe_free, 2)
            sp.wait_ge(pool_init, 2)
            for e in range(E):
                sp.dma_start(W2[:, e, 0:2, :], W2_d[e, 0:2 * P].rearrange("(k p) n -> p k n", p=P)).then_inc(loaded["W2"], 16)
                sp.dma_start(W2[0:H - 2 * P, e, 2, :], W2_d[e, 2 * P:H]).then_inc(loaded["W2"], 16)
            sp.wait_ge(scattered, 16 * NT)
            sp.dma_start(xd, xd_d.rearrange("(e s) d -> s e d", e=E)).then_inc(loaded["xd_rows"], 16)
            for part in range(4):
                cols = slice(part * 1280, (part + 1) * 1280)
                sp.dma_start(wqkv[:, :, cols], wqkv_d[:, cols].rearrange("(k p) n -> p k n", p=P)).then_inc(loaded["wqkv"], 16)
            for e in range(E):
                taken(sp, ("eout", e))
                sp.dma_start(oe_d[e * CAP:(e + 1) * CAP, :], oe[:, e, :]).then_inc(oe_stored, 16)
            landed(sp, ("eout", E - 1))
            sp.dma_start(wo, wo_d.rearrange("(h p) n -> p h n", p=P)).then_inc(loaded["wo"], 16)
            sp.dma_start(wgate, wgate_d.rearrange("(k p) n -> p k n", p=P)).then_inc(loaded["wffn"], 16)
            sp.dma_start(wup, wup_d.rearrange("(k p) n -> p k n", p=P)).then_inc(loaded["wffn"], 16)
            sp.dma_start(wdown, wdown_d.rearrange("(k p) n -> p k n", p=P)).then_inc(loaded["wffn"], 16)
            for i in range(NT):
                sp.wait_ge(x_out, i + 1)
                sp.dma_start(out_d[0, i * P:(i + 1) * P, :], x[:, i, :]).then_inc(stored, 16)
            sp.wait_ge(stored, 16 * NT)

        @block.tensor
        def _(pe):
            order = iter(plan.turn)

            def claim(job):
                assert next(order) == job, job
                slot, n = plan.turn[job]
                if n:
                    pe.wait_ge(drained[slot], n)
                return bank(job)

            def mm(out, lhsT, rhs, start=True, stop=True):
                return nc.tensor.matmul(out, lhsT=lhsT, rhs=rhs, start=start, stop=stop)

            pe.wait_ge(sc_ready, 1)
            pe.wait_ge(loaded["wmod"], 32)
            ps = claim(("modcol",))
            for l in range(2):
                for j, at in enumerate((0, 128, 256, 384, 768, 896, 1024, 1152)):
                    for k in range(KD):
                        last = mm(ps[:, l * 8 + j:l * 8 + j + 1], wmod[:, l, k, at:at + P],
                                  small[:, 2 * l + k:2 * l + k + 1], k == 0, k == KD - 1)
            last.then_inc(is_filled(("modcol",)), 1)
            pe.wait_ge(scb_ready, 1)
            for l in range(2):
                ps = claim(("modrow", l))
                for j, at in enumerate((512, 1280)):
                    for k in range(KD):
                        last = mm(ps[:, j * D:(j + 1) * D], sc_b[:, 2 * l + k, :],
                                  wmod[:, l, k, at:at + D], k == 0, k == KD - 1)
                last.then_inc(is_filled(("modrow", l)), 1)

            def transpose_h(which):
                for g in range(NT // 2):
                    pe.wait_ge(ln_done, ln_no[which, 2 * g + 1] + 1)
                    ps = claim(("hT", which, g))
                    for k in range(KD):
                        for t in range(2):
                            last = nc.tensor.transpose(ps[:, k * D + t * P:k * D + (t + 1) * P],
                                                       xn[:, 2 * g + t, k * P:(k + 1) * P], ident)
                    last.then_inc(is_filled(("hT", which, g)), 1)

            transpose_h("mix")

            pe.wait_ge(loaded["W_in"], 16)
            for g in range(NT // 2):
                taken(pe, ("hT", "mix", g))
            ps = claim(("dt",))
            for i in range(NT):
                for k in range(KD):
                    last = mm(ps[:, i * NH:(i + 1) * NH], hT[:, k, i * P:(i + 1) * P],
                              W_in[:, k, 1152:1156], k == 0, k == KD - 1)
            last.then_inc(is_filled(("dt",)), 1)
            for n in range(2):
                for m in range(5):
                    ps = claim(("xbc", n, m))
                    for k in range(KD):
                        last = mm(ps, W_in[:, k, DI + m * P:DI + (m + 1) * P],
                                  hT[:, k, n * 512:(n + 1) * 512], k == 0, k == KD - 1)
                    last.then_inc(is_filled(("xbc", n, m)), 1)
                for i in range(4 * n, 4 * n + 4):
                    ps = claim(("z", i))
                    for k in range(KD):
                        last = mm(ps, hT[:, k, i * P:(i + 1) * P], W_in[:, k, 0:DI], k == 0, k == KD - 1)
                    last.then_inc(is_filled(("z", i)), 1)

            def front(c):
                cols = slice(c * P, (c + 1) * P)
                pe.wait_ge(conv_silu, 5 * (c // 4) + 5)
                ps = claim(("xtok", c))
                for m in range(4):
                    last = nc.tensor.transpose(ps[:, m * P:(m + 1) * P], xT[:, m, cols], ident)
                last.then_inc(is_filled(("xtok", c)), 1)
                ps = claim(("misc", c))
                pe.wait_ge(dt_ready, 1)
                nc.tensor.transpose(ps[:, 0:NS], BT[0:NS, cols], ident[0:NS, 0:NS])
                mm(ps[:, P:2 * P], BT[0:NS, cols], CT[0:NS, cols])
                mm(ps[:, 256:260], tri, a_dt(c))
                mm(ps[:, 260:264], ones[:, :], a_dt(c)).then_inc(is_filled(("misc", c)), 1)
                ps = claim(("seg", c))
                pe.wait_ge(m1_ready, c + 1)
                for h in range(NH):
                    last = mm(ps[:, h * P:(h + 1) * P], M1[:, c % 2, h, :], tri)
                last.then_inc(is_filled(("seg", c)), 1)

            pe.wait_ge(loaded["W_out"], 16)
            front(0)
            for c in range(NT):
                cols = slice(c * P, (c + 1) * P)
                ps = claim(("yoff", c))
                if c:
                    taken(pe, ("state", c - 1))
                else:
                    pe.wait_ge(pool_init, 1)
                mm(ps, CT[0:NS, cols], S[0:NS, c % 2].rearrange("p h d -> p (h d)")).then_inc(is_filled(("yoff", c)), 1)
                ps = claim(("ydiag", c))
                pe.wait_ge(mt_ready, c + 1)
                pe.wait_ge(xdt_ready, 2 * c + 2)
                for h in range(NH):
                    last = mm(ps[:, h * P:(h + 1) * P], MT[:, c % 2, h, :], Xdt[:, c % 2, h, :])
                last.then_inc(is_filled(("ydiag", c)), 1)
                ps = claim(("state", c))
                pe.wait_ge(xs_ready, c + 1)
                pe.wait_ge(misc_act, c + 1)
                mm(ps[0:NS, :], B_tok[:, c % 2, :], Xs[:, c % 2].rearrange("p h d -> p (h d)")).then_inc(is_filled(("state", c)), 1)
                if c + 1 < NT:
                    front(c + 1)
                ps = claim(("ygT", c))
                pe.wait_ge(yg_ready, c + 1)
                for m in range(4):
                    last = nc.tensor.transpose(ps[:, m * P:(m + 1) * P], yg[:, m, :], ident)
                last.then_inc(is_filled(("ygT", c)), 1)
                ps = claim(("mixout", c))
                taken(pe, ("ygT", c))
                for k in range(4):
                    last = mm(ps[:, 0:D], ygT[:, k, :], W_out[:, k, :], k == 0, k == 3)
                last.then_inc(is_filled(("mixout", c)), 1)

            transpose_h("moe")
            pe.wait_ge(loaded["Wg"], 16)
            for g in range(NT // 2):
                taken(pe, ("hT", "moe", g))
            ps = claim(("logits",))
            for i in range(NT):
                for k in range(KD):
                    last = mm(ps[:, i * E:(i + 1) * E], hT[:, k, i * P:(i + 1) * P], Wg[:, k, :],
                              k == 0, k == KD - 1)
            last.then_inc(is_filled(("logits",)), 1)
            ps = claim(("rank",))
            pe.wait_ge(oh_ready, 1)
            mm(ps[:, 0:64], tri, route[:, 2, :], True, False)
            mm(ps[:, 0:64], ones[:, :], route[:, 3, :], False, True).then_inc(is_filled(("rank",)), 1)
            pe.wait_ge(loaded["sw"], 64)
            for n in range(2):
                for m in range(KH):
                    for name, w in (("sh1", sw1), ("sh3", sw3)):
                        ps = claim((name, n, m))
                        for k in range(KD):
                            last = mm(ps, w[:, k, m * P:(m + 1) * P], hT[:, k, n * 512:(n + 1) * 512],
                                      k == 0, k == KD - 1)
                        last.then_inc(is_filled((name, n, m)), 1)
                for i in range(4 * n, 4 * n + 4):
                    ps = claim(("shout", i))
                    taken(pe, ("sh3", n, KH - 1))
                    for m in range(KH):
                        last = mm(ps[:, 0:D], hs[:, m, i * P:(i + 1) * P], sw2[:, m, :], m == 0, m == KH - 1)
                    last.then_inc(is_filled(("shout", i)), 1)
            pe.wait_ge(loaded["xd_rows"], 16)
            for g in range(4):
                ps = claim(("xdT", g))
                for k in range(KD):
                    for t in range(2):
                        last = nc.tensor.transpose(ps[:, k * D + t * P:k * D + (t + 1) * P],
                                                   xd[:, 2 * g + t, k * P:(k + 1) * P], ident)
                last.then_inc(is_filled(("xdT", g)), 1)

            def expert_up(e):
                pe.wait_ge(loaded["W1"], 16 * E)
                pe.wait_ge(loaded["W3"], 16 * E)
                taken(pe, ("xdT", e // 2))
                for name, w in (("e1", W1), ("e3", W3)):
                    ps = claim((name, e))
                    for m in range(KH):
                        for k in range(KD):
                            last = mm(ps[:, m * P:(m + 1) * P], w[:, e, k, m * P:(m + 1) * P],
                                      xdT[:, k, e, :], k == 0, k == KD - 1)
                    last.then_inc(is_filled((name, e)), 1)

            expert_up(0)
            for e in range(E):
                if e + 1 < E:
                    expert_up(e + 1)
                ps = claim(("eout", e))
                pe.wait_ge(loaded["W2"], 32 * E)
                taken(pe, ("e3", e))
                for m in range(KH):
                    last = mm(ps[:, 0:D], he[:, e % 2, m * P:(m + 1) * P], W2[:, e, m, :], m == 0, m == KH - 1)
                last.then_inc(is_filled(("eout", e)), 1)

            pe.wait_ge(x_moe, NT)
            pe.wait_ge(loaded["wqkv"], 64)

            def scores(i, h):
                ps = claim(("S", i, h))
                g = h // REP
                taken(pe, ("qkT", i, g))
                if h == 0:
                    taken(pe, ("qkT", i, "k"))
                n = (i + 1) * P
                for at in range(0, n, 512):
                    end = min(at + 512, n)
                    last = mm(ps[:, at:end], qT[:, h, :], kT[:, g, at:end], True, end < n)
                mm(ps[:, i * P:n], ident_h[:, :], mask_h[:, :], False, True).then_inc(is_filled(("S", i, h)), 1)

            def project(job, w_at, lhs):
                ps = claim(job)
                for k in range(KD):
                    last = mm(ps, lhs[:, k, :], wqkv[:, k, w_at:w_at + 512], k == 0, k == KD - 1)
                last.then_inc(is_filled(job), 1)

            def beside_pe(work):
                kind, i, *rest = work
                if kind == "h3T":
                    pe.wait_ge(ln_done, ln_no["ln3", i] + 1)
                    ps = claim(work)
                    for k in range(KD):
                        last = nc.tensor.transpose(ps[:, k * P:(k + 1) * P], xn1[:, 0, k * P:(k + 1) * P], ident)
                    last.then_inc(is_filled(work), 1)
                elif kind == "h4T":
                    pe.wait_ge(ln_done, ln_no["ln4", i] + 1)
                    ps = claim(work)
                    for k in range(KD):
                        last = nc.tensor.transpose(ps[:, k * P:(k + 1) * P], xn1[:, 1, k * P:(k + 1) * P], ident)
                    last.then_inc(is_filled(work), 1)
                elif kind == "proj":
                    taken(pe, ("h3T", i))
                    c = rest[0]
                    project(work, {"k": 4096, "v": 4608}.get(c, 0) if c in ("k", "v") else c * 512, h3T[:, i % 2])
                elif kind == "gate":
                    taken(pe, ("h3T", i))
                    project(work, 2048 + rest[0] * 512, h3T[:, i % 2])
                elif kind == "eT":
                    pe.wait_ge(tab_ready, i + 1)
                    ps = claim(work)
                    for a in range(2):
                        last = nc.tensor.transpose(ps[:, a * P:(a + 1) * P], rope_E[:, a, :], ident)
                    last.then_inc(is_filled(work), 1)
                elif kind == "qkT":
                    r_no = rope_no[i, rest[0]]
                    pe.wait_ge(rope_r, r_no + 1)
                    pe.wait_ge(rope_i, r_no + 1)
                    ps = claim(work)
                    for a in range(4):
                        last = nc.tensor.transpose(ps[:, a * P:(a + 1) * P], roped_of(r_no)[:, a, :], ident)
                    last.then_inc(is_filled(work), 1)
                elif kind == "oT":
                    g = rest[0]
                    taken(pe, ("O", i, 4 * g + 3))
                    ps = claim(work)
                    for a in range(4):
                        last = nc.tensor.transpose(ps[:, a * P:(a + 1) * P], osb[:, a * P:(a + 1) * P], ident)
                    last.then_inc(is_filled(work), 1)
                elif kind == "wo":
                    if i == 0:
                        pe.wait_ge(loaded["wo"], 16)
                    for g in range(4):
                        taken(pe, ("oT", i, g))
                    ps = claim(work)
                    for h in range(HQ):
                        last = mm(ps[:, 0:D], oT[:, h, :], wo[:, h, :], h == 0, h == HQ - 1)
                    last.then_inc(is_filled(work), 1)
                elif kind == "gu":
                    c = rest[0]
                    if i == 0 and c == 0:
                        pe.wait_ge(loaded["wffn"], 48)
                    taken(pe, ("h4T", i))
                    w = (wgate, wup)[c % 2]
                    ps = claim(work)
                    for k in range(KD):
                        last = mm(ps, h4T[:, k, :], w[:, k, c // 2 * 512:(c // 2 + 1) * 512], k == 0, k == KD - 1)
                    last.then_inc(is_filled(work), 1)
                elif kind == "hsT":
                    g = rest[0]
                    pe.wait_ge(sparse_ready, sparse_no(i))
                    ps = claim(work)
                    for a in range(4):
                        b = 4 * g + a
                        last = nc.tensor.transpose(ps[:, a * P:(a + 1) * P], sg[:, b * P:(b + 1) * P], ident)
                    last.then_inc(is_filled(work), 1)
                elif kind == "down":
                    for g in range(2):
                        taken(pe, ("hsT", i, g))
                    ps = claim(work)
                    for m in range(FF // P):
                        last = mm(ps[:, 0:D], hsT[:, m, :], wdown[:, m, :], m == 0, m == FF // P - 1)
                    last.then_inc(is_filled(work), 1)

            for att, beside in steps:
                if att == (0, 0):
                    for h in range(AHEAD):
                        scores(0, h)
                if att:
                    i, h = att
                    taken(pe, ("S", i, h))
                    for g, js in enumerate(groups(i)):
                        ps = claim(("PT", i, h, g))
                        for a, j in enumerate(js):
                            last = nc.tensor.transpose(ps[:, a * P:(a + 1) * P], pr[:, h % 2, j * P:(j + 1) * P], ident)
                        last.then_inc(is_filled(("PT", i, h, g)), 1)
                if att and after(att):
                    scores(*after(att))
                for work in beside:
                    beside_pe(work)
                if att:
                    ps = claim(("O", i, h))
                    if h == 0:
                        taken(pe, ("proj", i, "v"))
                    for g, js in enumerate(groups(i)):
                        taken(pe, ("PT", i, h, g))
                        for a, j in enumerate(js):
                            last = mm(ps[:, 0:DH], PT[:, pt_no[i, h, g] % 2, a * P:(a + 1) * P],
                                      v[:, j, h // REP * DH:(h // REP + 1) * DH], j == 0, j == i)
                    last.then_inc(is_filled(("O", i, h)), 1)
            assert next(order, None) is None

        @block.scalar
        def _(eng):
            marks = [0]

            def mark(ins):
                marks[0] += 1
                ins.then_inc(act, 1)

            def own():
                eng.wait_ge(act, marks[0])

            ac = nc.scalar.activation
            eng.wait_ge(loaded["vectors"], 16)
            ac(small[:, 0:4], c_cols, ACT.Silu).then_inc(sc_ready, 1)

            def h_modulated(which, shift, scale):
                for g in range(NT // 2):
                    job = ("hT", which, g)
                    landed(eng, job)
                    for k in range(KD):
                        last = ac(hT[:, k, g * D:(g + 1) * D], bank(job)[:, k * D:(k + 1) * D], ACT.Identity,
                                  bias=mod_col[:, shift + k:shift + k + 1], scale=mod_col[:, scale + k:scale + k + 1])
                    last.then_inc(is_drained(job), 1)

            taken(eng, ("modcol",))
            h_modulated("mix", 0, 2)

            def conv_act(n, m):
                if (n, m) == (0, 0):
                    eng.wait_ge(pool_init, 1)
                job = ("xbc", n, m)
                landed(eng, job)
                ac(xc[:, m, 3 + n * 512:3 + (n + 1) * 512], bank(job), ACT.Copy).then_inc(conv_in, 1)
                ac(xT[:, m, n * 512:(n + 1) * 512], bank(job), ACT.Copy, scale=conv_w[:, m, 3:4]).then_inc(is_drained(job), 1)

            def conv_silu_act(n, m):
                cols = slice(n * 512, (n + 1) * 512)
                eng.wait_ge(conv_done, 5 * n + m + 1)
                if m < 4:
                    ac(xT[:, m, cols], xT[:, m, cols], ACT.Silu, bias=conv_b[:, m:m + 1]).then_inc(conv_silu, 1)
                else:
                    ac(BT[0:NS, cols], xT[0:NS, m, cols], ACT.Silu, bias=conv_b[0:NS, m:m + 1])
                    ac(CT[0:NS, cols], xT[NS:P, m, cols], ACT.Silu, bias=conv_b[NS:P, m:m + 1]).then_inc(conv_silu, 1)

            for n in range(2):
                for m in range(5):
                    conv_act(n, m)
                    if m:
                        conv_silu_act(n, m - 1)
                for i in range(4 * n, 4 * n + 4):
                    landed(eng, ("z", i))
                    ac(zs[:, i, :], bank(("z", i)), ACT.Silu).then_inc(is_drained(("z", i)), 1)
                    if i == 4 * n:
                        conv_silu_act(n, 4)

            ac(small[:, 4:8], a_log, ACT.Exp).then_inc(a_exp, 1)
            eng.wait_ge(dt_abs, 1)
            ac(dtb[:, 2, :], dtb[:, 1, :], ACT.Exp, scale=-1.0).then_inc(dt_exp, 1)

            def front(c):
                if c:
                    eng.wait_ge(xdt_ready, 2 * c)
                landed(eng, ("xtok", c))
                ac(x_sb, bank(("xtok", c)).rearrange("p (h d) -> p h d", h=NH), ACT.Copy).then_inc(is_drained(("xtok", c)), 1)
                if c >= 2:
                    taken(eng, ("state", c - 2))
                landed(eng, ("misc", c))
                ac(es[:, c % 2, :], bank(("misc", c))[:, 256:264], ACT.Exp)
                ac(B_tok[:, c % 2, :], bank(("misc", c))[:, 0:NS], ACT.Copy).then_inc(misc_act, 1)
                if c:
                    eng.wait_ge(xs_ready, c)
                landed(eng, ("seg", c))
                ac(Lm, bank(("seg", c)).rearrange("p (h d) -> p h d", h=NH), ACT.Exp).then_inc(is_drained(("seg", c)), 1)

            front(0)
            for c in range(NT):
                if c + 1 < NT:
                    front(c + 1)
                eng.wait_ge(yg_ready, c + 1)
                ac(sq_out, yg.rearrange("p h d -> p (h d)"), ACT.Square, accum_out=small[:, 8 + c:9 + c]).then_inc(yg_sq, 1)
            eng.wait_ge(x_mixed, NT)
            ac(small[:, 40:41], small[:, 8:9], ACT.Copy).then_inc(moe_free, 1)

            h_modulated("moe", 4, 6)
            eng.wait_ge(route_d, 1)
            ac(route[:, 4, :], route[:, 1, :], ACT.Exp).then_inc(route_e, 1)
            for n in range(2):
                for m in range(KH):
                    u = KH * n + m
                    if u >= 2:
                        taken(eng, ("sh3", (u - 2) // KH, (u - 2) % KH))
                    landed(eng, ("sh1", n, m))
                    ac(s1[:, u % 2, :], bank(("sh1", n, m)), ACT.Silu).then_inc(is_drained(("sh1", n, m)), 1)
            for g in range(4):
                job = ("xdT", g)
                landed(eng, job)
                for k in range(KD):
                    last = ac(xdT[:, k, 2 * g:2 * g + 2, :], bank(job)[:, k * D:(k + 1) * D].rearrange("p (e s) -> p e s", e=2),
                              ACT.Identity, bias=mod_col[:, 4 + k:5 + k], scale=mod_col[:, 6 + k:7 + k])
                last.then_inc(is_drained(job), 1)

            def expert_act(e):
                if e >= 2:
                    taken(eng, ("e3", e - 2))
                landed(eng, ("e1", e))
                ac(se[:, e % 2, :], bank(("e1", e))[:, 0:HP], ACT.Silu).then_inc(is_drained(("e1", e)), 1)

            expert_act(0)
            for e in range(E):
                if e + 1 < E:
                    expert_act(e + 1)
                landed(eng, ("eout", e))
                ac(oe[:, e, :], bank(("eout", e))[:, 0:D], ACT.Copy).then_inc(is_drained(("eout", e)), 1)

            eng.wait_ge(x_moe, NT)

            def softmax(i, h):
                no = i * HQ + h
                n = (i + 1) * P
                landed(eng, ("S", i, h))
                eng.wait_ge(maxed, no + 1)
                if no >= 2:
                    pi, ph = divmod(no - 2, HQ)
                    landed(eng, ("PT", pi, ph, len(groups(pi)) - 1))
                if no >= 4:
                    taken(eng, ("O", *divmod(no - 4, HQ)))
                ac(pr[:, h % 2, 0:n], bank(("S", i, h))[:, 0:n], ACT.Exp, bias=nmax[:, no % 4:no % 4 + 1],
                   accum_out=rsum[:, no % 4:no % 4 + 1]).then_inc(is_drained(("S", i, h)), 1)

            def beside_act(work):
                kind, i, *rest = work
                ps = bank(work) if work in plan.turn else None
                if kind == "h3T":
                    if i >= 2:
                        landed(eng, ("gate", i - 2, 3))
                    landed(eng, work)
                    for k in range(KD):
                        last = ac(h3T[:, i % 2, k, :], ps[:, k * P:(k + 1) * P], ACT.Identity,
                                  bias=mod_col[:, 8 + k:9 + k], scale=mod_col[:, 10 + k:11 + k])
                    last.then_inc(is_drained(work), 1)
                elif kind == "h4T":
                    if i:
                        landed(eng, ("gu", i - 1, 3))
                    landed(eng, work)
                    for k in range(KD):
                        last = ac(h4T[:, k, :], ps[:, k * P:(k + 1) * P], ACT.Identity,
                                  bias=mod_col[:, 12 + k:13 + k], scale=mod_col[:, 14 + k:15 + k])
                    last.then_inc(is_drained(work), 1)
                elif kind == "proj" and rest[0] == "v":
                    landed(eng, work)
                    ac(v[:, i, :], ps, ACT.Copy).then_inc(is_drained(work), 1)
                elif kind == "proj":
                    r_no = rope_no[i, rest[0]]
                    if r_no > 4:
                        eng.wait_ge(rope_r, r_no)
                        eng.wait_ge(rope_i, r_no)
                    landed(eng, work)
                    ac(raw_of(r_no), ps.rearrange("p (h d) -> p h d", h=4), ACT.Copy).then_inc(is_drained(work), 1)
                elif kind == "gate":
                    no = 4 * i + rest[0]
                    if no >= 2:
                        pi, pg = divmod(no - 2, 4)
                        taken(eng, ("O", pi, 4 * pg + 3))
                    landed(eng, work)
                    ac(gate[:, no % 2, :], ps, ACT.Tanh, scale=0.5).then_inc(is_drained(work), 1)
                elif kind == "eT":
                    if i:
                        taken(eng, ("qkT", i - 1, 3))
                    landed(eng, work)
                    ac(eT, ps[:, 0:D].rearrange("p (a t) -> p a t", a=2), ACT.Copy).then_inc(is_drained(work), 1)
                elif kind == "oT":
                    g = rest[0]
                    if i:
                        landed(eng, ("wo", i - 1))
                    landed(eng, work)
                    ac(oT[:, 4 * g:4 * g + 4, :], ps.rearrange("p (h t) -> p h t", h=4), ACT.Copy).then_inc(is_drained(work), 1)
                elif kind == "gu" and rest[0] % 2 == 0:
                    half = rest[0] // 2
                    if i:
                        eng.wait_ge(sparse_ready, sparse_no(i - 1))
                    landed(eng, work)
                    ac(tb[:, half * 512:(half + 1) * 512], ps, ACT.Tanh, scale=0.5).then_inc(gu_tanh, 1)
                elif kind == "hsT":
                    g = rest[0]
                    if i:
                        landed(eng, ("down", i - 1))
                    landed(eng, work)
                    ac(hsT[:, 4 * g:4 * g + 4, :], ps.rearrange("p (h t) -> p h t", h=4), ACT.Copy).then_inc(is_drained(work), 1)

            for att, beside in steps:
                if att == (0, 0):
                    for h in range(AHEAD):
                        softmax(0, h)
                if att:
                    i, h = att
                    no = pt_no[i, h, 0]
                    if no >= 2:
                        landed(eng, ("O", *pt_key[no - 2][:2]))
                    n = len(groups(i)[0]) * P
                    landed(eng, ("PT", i, h, 0))
                    ac(PT[:, no % 2, 0:n], bank(("PT", i, h, 0))[:, 0:n], ACT.Copy).then_inc(is_drained(("PT", i, h, 0)), 1)
                if att and after(att):
                    softmax(*after(att))
                for work in beside:
                    beside_act(work)

        @block.vector
        def _(eng):
            marks = [0]

            def mark(ins):
                marks[0] += 1
                ins.then_inc(dve, 1)

            def own():
                eng.wait_ge(dve, marks[0])

            ts, tt, stt = nc.vector.tensor_scalar, nc.vector.tensor_tensor, nc.vector.scalar_tensor_tensor

            nc.vector.memset(ones[:, :], 1.0)
            nc.vector.memset(half_neg[:, :], -0.5)
            nc.vector.memset(zeros, 0.0).then_inc(dve_init, 1)
            eng.wait_ge(dve_init, 1)
            eng.wait_ge(loaded["consts"], 16)
            mark(nc.vector.tensor_copy(ident_h[:, :], ident))
            mark(tt(xtmp[:, 0:P], tri, ident, ALU.subtract))
            own()
            mark(ts(mask_h[:, :], xtmp[:, 0:P], MASKED, None, ALU.mult))
            eng.wait_ge(sc_ready, 1)
            for s in range(4):
                last = ts(sc_b[:, s, :], ones[:, :], small[:, s:s + 1], None, ALU.mult)
            last.then_inc(scb_ready, 1)

            def stats(key, i):
                s = ln_no[key, i] % 4
                if ln_no[key, i] >= 4:
                    eng.wait_ge(ln_done, ln_no[key, i] - 3)
                mark(nc.vector.bn_stats(ln_st[:, s, :], x[:, i, :]))
                own()
                nc.vector.bn_aggr(ln_mv[:, s, :], ln_st[:, s, :]).then_inc(ln_stats, 1)

            def normalise(key, i, out):
                n = ln_no[key, i]
                eng.wait_ge(ln_scaled, n + 1)
                eng.wait_ge(ln_stats, n + 1)
                ts(out, x[:, i, :], ln_mv[:, n % 4, 0:1], ln_rstd[:, n % 4:n % 4 + 1],
                   ALU.subtract, ALU.mult).then_inc(ln_done, 1)

            eng.wait_ge(loaded["x"], 16)
            for i in range(NT + 2):
                if i < NT:
                    stats("mix", i)
                if i >= 2:
                    normalise("mix", i - 2, xn[:, i - 2, :])

            landed(eng, ("modcol",))
            mark(nc.vector.tensor_copy(mod_col[:, :], bank(("modcol",))[:, 0:16]))
            own()
            mc = mod_col[:, :].rearrange("p (s v k) -> p s v k", s=4, v=2)
            ts(mc[:, :, 1, :], mc[:, :, 1, :], 1.0, None, ALU.add).then_inc(is_drained(("modcol",)), 1)
            for l in range(2):
                job = ("modrow", l)
                landed(eng, job)
                nc.vector.tensor_copy(g_row[:, l, :], bank(job)).then_inc(is_drained(job), 1)
                taken(eng, job)
                mark(stt(g_abs, g_row[:, l, :], -1.0, g_row[:, l, :], ALU.mult, ALU.max))
                own()
                mark(ts(g_abs, g_abs, 0.25, None, ALU.max))
                mark(ts(g_row[:, l, :], g_row[:, l, :], 0.0, 2.0, ALU.is_ge, ALU.mult))
                own()
                stt(g_row[:, l, :], g_row[:, l, :], -1.0, g_abs, ALU.add, ALU.mult).then_inc(g_ready, 1)
                eng.wait_ge(g_ready, l + 1)

            job = ("dt",)
            landed(eng, job)
            bc8 = lambda t: t.unsqueeze(1).to_broadcast([P, NT, NH])
            d3 = lambda n: dtb[:, n, :].rearrange("p (i h) -> p i h", h=NH)
            tt(d3(0), bank(job)[:, 0:32].rearrange("p (i h) -> p i h", h=NH), bc8(dt_bias),
               ALU.add).then_inc(is_drained(job), 1)
            taken(eng, job)
            stt(dtb[:, 1, :], dtb[:, 0, :], -1.0, dtb[:, 0, :], ALU.mult, ALU.max).then_inc(dt_abs, 1)

            def conv(n, m):
                eng.wait_ge(conv_in, 5 * n + m + 1)
                taken(eng, ("xbc", n, m))
                acc = xT[:, m, n * 512:(n + 1) * 512]
                for j in range(3):
                    ins = stt(acc, xc[:, m, n * 512 + j:n * 512 + j + 512], conv_w[:, m, j:j + 1], acc, ALU.mult, ALU.add)
                    if j < 2:
                        mark(ins)
                        own()
                ins.then_inc(conv_done, 1)

            for n in range(2):
                for m in range(5):
                    conv(n, m)

            eng.wait_ge(dt_exp, 1)
            ts(dt_as_relu, dtb[:, 0, :], 0.0, None, ALU.max)
            mark(ts(dtb[:, 3, :], dtb[:, 2, :], 2.0, None, ALU.add))
            own()
            mark(nc.vector.reciprocal(dtb[:, 4, :], dtb[:, 3, :]))
            own()
            mark(tt(dtb[:, 5, :], dtb[:, 4, :], dtb[:, 2, :], ALU.mult))
            own()
            mark(tt(dtb[:, 6, :], dtb[:, 5, :], dtb[:, 5, :], ALU.mult))
            own()
            mark(ts(dtb[:, 7, :], dtb[:, 6, :], 1.0 / 17, None, ALU.mult))
            for d in (15, 13, 11, 9, 7, 5, 3):
                own()
                mark(stt(dtb[:, 7, :], dtb[:, 7, :], 1.0 / d, dtb[:, 6, :], ALU.add, ALU.mult))
            own()
            mark(stt(dtb[:, 7, :], dtb[:, 7, :], 1.0, dtb[:, 5, :], ALU.add, ALU.mult))
            own()
            mark(stt(dtb[:, 9, :], dtb[:, 7, :], 2.0, dt_as_relu, ALU.mult, ALU.add))
            own()
            eng.wait_ge(a_exp, 1)
            stt(d3(10), d3(9), -1.0, bc8(small[:, 4:8]), ALU.mult, ALU.mult).then_inc(dt_ready, 1)

            def over_heads(t):
                return t.unsqueeze(1).to_broadcast([P, NH, P])

            def front(c):
                b = c % 2
                job = ("misc", c)
                landed(eng, job)
                eng.wait_ge(misc_act, c + 1)
                if c:
                    eng.wait_ge(mt_ready, c)
                tt(Gm, bank(job)[:, P:2 * P], tri, ALU.mult).then_inc(is_drained(job), 1)
                taken(eng, job)
                taken(eng, ("seg", c))
                tt(MT[:, b], Lm, over_heads(Gm), ALU.mult).then_inc(mt_ready, 1)
                eng.wait_ge(xdt_ready, 2 * c + 2)
                tt(Xs[:, b], Xdt[:, b], Lm[:, :, P - 1].unsqueeze(2).to_broadcast([P, NH, P]), ALU.mult).then_inc(xs_ready, 1)

            front(0)
            for c in range(NT):
                b = c % 2
                if c:
                    eng.wait_ge(yg_ready, c)
                job = ("ydiag", c)
                landed(eng, job)
                tt(y1, bank(job).rearrange("p (h d) -> p h d", h=NH), xD[:, b], ALU.add).then_inc(is_drained(job), 1)
                taken(eng, job)
                job = ("yoff", c)
                landed(eng, job)
                for h in range(NH):
                    last = stt(y1[:, h, :], bank(job)[:, h * P:(h + 1) * P], es[:, b, h:h + 1], y1[:, h, :], ALU.mult, ALU.add)
                last.then_inc(is_drained(job), 1)
                job = ("state", c)
                landed(eng, job)
                if c:
                    taken(eng, ("state", c - 1))
                for h in range(NH):
                    last = stt(S[0:NS, 1 - b, h, :], S[0:NS, b, h, :], es[0:NS, b, 4 + h:5 + h],
                               bank(job)[0:NS, h * P:(h + 1) * P], ALU.mult, ALU.add)
                last.then_inc(is_drained(job), 1)
                if c + 1 < NT:
                    front(c + 1)
                job = ("ygT", c)
                landed(eng, job)
                if c == 0:
                    eng.wait_ge(zeroed, 16)
                tt(ygT, bank(job).rearrange("p (k t) -> p k t", k=4), norm_w.unsqueeze(2).to_broadcast([P, 4, P]),
                   ALU.mult).then_inc(is_drained(job), 1)
                job = ("mixout", c)
                landed(eng, job)
                eng.wait_ge(yg_rstd, c + 1)
                stt(xtmp[:, :], bank(job)[:, 0:D], small[:, 24 + c:25 + c], g_row[:, 0, 0:D], ALU.mult, ALU.mult).then_inc(is_drained(job), 1)
                taken(eng, job)
                tt(x[:, c, :], x[:, c, :], xtmp[:, :], ALU.add).then_inc(x_mixed, 1)
            eng.wait_ge(x_mixed, NT)
            eng.wait_ge(moe_free, 2)

            for i in range(NT + 2):
                if i < NT:
                    stats("moe", i)
                if i >= 2:
                    normalise("moe", i - 2, xn[:, i - 2, :])
            r3 = lambda n: route[:, n, :].rearrange("p (i e) -> p i e", e=E)
            over_e = lambda n: rt8[:, n, :].unsqueeze(2).to_broadcast([P, NT, E])
            job = ("logits",)
            landed(eng, job)
            lg = bank(job)[:, 0:64].rearrange("p (i e) -> p i e", e=E)
            mark(nc.vector.reduce_max(rt8[:, 0, :], lg, AX_X))
            own()
            mark(tt(r3(0), lg, over_e(0), ALU.is_equal))
            tt(r3(1), lg, over_e(0), ALU.subtract).then_inc(is_drained(job), 1)
            taken(eng, job)
            nc.vector.tensor_copy(rt8[:, 8, :], rt8[:, 0, :]).then_inc(route_d, 1)
            own()
            mark(tt(route[:, 0, :], route[:, 0, :], rank_weight, ALU.mult))
            own()
            mark(nc.vector.reduce_max(rt8[:, 1, :], r3(0), AX_X))
            own()
            mark(tt(r3(2), r3(0), over_e(1), ALU.is_equal))
            mark(nc.vector.memset(route[:, 3, 0:E], 0.0))
            own()
            for i in range(1, NT):
                ins = tt(route[:, 3, i * E:(i + 1) * E], route[:, 3, (i - 1) * E:i * E],
                         route[:, 2, (i - 1) * E:i * E], ALU.add)
                if i < NT - 1:
                    mark(ins)
                    own()
            ins.then_inc(oh_ready, 1)
            job = ("rank",)
            landed(eng, job)
            eng.wait_ge(oh_ready, 1)
            tt(route[:, 0, :], bank(job)[:, 0:64], route[:, 2, :], ALU.mult).then_inc(is_drained(job), 1)
            taken(eng, job)
            mark(nc.vector.reduce_sum(rt8[:, 2, :], r3(0), AX_X))
            mark(tt(route[:, 3, :], route[:, 2, :], expert_base, ALU.mult))
            own()
            mark(nc.vector.reduce_sum(rt8[:, 3, :], r3(3), AX_X))
            mark(ts(rt8[:, 4, :], rt8[:, 2, :], CAP + 0.5, None, ALU.is_le))
            eng.wait_ge(route_e, 1)
            mark(nc.vector.reduce_sum(rt8[:, 5, :], r3(4), AX_X))
            own()
            mark(stt(rt8[:, 3, :], rt8[:, 2, :], -1.0, rt8[:, 3, :], ALU.add, ALU.add))
            mark(ts(rt8[:, 6, :], rt8[:, 4, :], -NEVER, NEVER, ALU.mult, ALU.add))
            mark(nc.vector.reciprocal(rt8[:, 5, :], rt8[:, 5, :]))
            own()
            mark(tt(rt8[:, 6, :], rt8[:, 6, :], rt8[:, 3, :], ALU.add))
            mark(tt(rt8[:, 7, :], rt8[:, 5, :], rt8[:, 4, :], ALU.mult))
            own()
            mark(nc.vector.tensor_copy(slot_u[:, 0, :], rt8[:, 6, :]))
            ts(slot_u[:, 1, :], rt8[:, 6, :], float(E * CAP - 1), None, ALU.min).then_inc(route_done, 1)

            for n in range(2):
                for m in range(KH):
                    u = KH * n + m
                    job = ("sh3", n, m)
                    landed(eng, job)
                    taken(eng, ("sh1", n, m))
                    tt(hs[:, m, n * 512:(n + 1) * 512], bank(job), s1[:, u % 2, :], ALU.mult).then_inc(is_drained(job), 1)
                for i in range(4 * n, 4 * n + 4):
                    job = ("shout", i)
                    landed(eng, job)
                    if i:
                        eng.wait_ge(x_shared, i)
                    tt(xtmp[:, :], bank(job)[:, 0:D], g_row[:, 0, D:2 * D], ALU.mult).then_inc(is_drained(job), 1)
                    taken(eng, job)
                    tt(x[:, i, :], x[:, i, :], xtmp[:, :], ALU.add).then_inc(x_shared, 1)
            for e in range(E):
                if e >= 2:
                    landed(eng, ("eout", e - 2))
                job = ("e3", e)
                landed(eng, job)
                taken(eng, ("e1", e))
                tt(he[:, e % 2, :], bank(job)[:, 0:HP], se[:, e % 2, :], ALU.mult).then_inc(is_drained(job), 1)
            own()
            eng.wait_ge(x_shared, NT)
            for i in range(NT):
                eng.wait_ge(gathered, 16 * NT)
                if i:
                    eng.wait_ge(x_moe, i)
                mark(stt(xtmp[:, :], og[:, i, :], rt8[:, 7, i:i + 1], g_row[:, 0, D:2 * D], ALU.mult, ALU.mult))
                own()
                tt(x[:, i, :], x[:, i, :], xtmp[:, :], ALU.add).then_inc(x_moe, 1)
            eng.wait_ge(x_moe, NT)

            def row_max(i, h):
                no = i * HQ + h
                landed(eng, ("S", i, h))
                if no >= 4:
                    taken(eng, ("S", *divmod(no - 4, HQ)))
                nc.vector.reduce_max(nmax[:, no % 4:no % 4 + 1], bank(("S", i, h))[:, 0:(i + 1) * P], AX_X,
                                     negate=True).then_inc(maxed, 1)

            def beside_dve(work):
                kind, i, *rest = work
                ps = bank(work) if work in plan.turn else None
                if kind in ("ln3", "ln4"):
                    if kind == "ln4":
                        eng.wait_ge(x_att, i + 1)
                    stats(kind, i)
                    if i:
                        landed(eng, ({"ln3": "h3T", "ln4": "h4T"}[kind], i - 1))
                    normalise(kind, i, xn1[:, 0 if kind == "ln3" else 1, :])
                elif kind == "proj" and rest[0] != "v":
                    r_no = rope_no[i, rest[0]]
                    taken(eng, work)
                    for a in range(4):
                        last = nc.vector.bn_stats(q_st[:, r_no % 2, a, :], raw_of(r_no)[:, a, :])
                    mark(last)
                    own()
                    for a in range(4):
                        last = nc.vector.bn_aggr(q_mv[:, r_no % 2, a, :], q_st[:, r_no % 2, a, :])
                    last.then_inc(q_stats, 1)
                elif kind == "rope":
                    r_no = rope_no[i, rest[0]]
                    b, qk = r_no % 2, int(rest[0] == "k")
                    eng.wait_ge(q_rstd, r_no + 1)
                    eng.wait_ge(q_stats, r_no + 1)
                    for a in range(4):
                        last = ts(raw_of(r_no)[:, a, :], raw_of(r_no)[:, a, :], q_mv[:, b, a, 0:1], q_rs[:, b, a:a + 1],
                                  ALU.subtract, ALU.mult)
                    last.then_inc(q_norm, 1)
                    eng.wait_ge(q_norm, r_no + 1)
                    eng.wait_ge(tab_ready, i + 1)
                    if r_no:
                        eng.wait_ge(rope_r, r_no)
                    table = lambda s: rt[:, s, qk, :].unsqueeze(1).to_broadcast([P, 4, 64])
                    mark(tt(t_r[:, 0], raw_of(r_no)[:, :, 0:64], table(0), ALU.mult))
                    mark(tt(t_r[:, 1], raw_of(r_no)[:, :, 64:128], table(1), ALU.mult))
                    own()
                    if r_no > 4:
                        pi, pc = divmod(r_no - 1, 5)
                        landed(eng, ("qkT", pi, ("k", 0, 1, 2, 3)[pc]))
                    tt(roped_of(r_no)[:, :, 0:64], t_r[:, 0], t_r[:, 1], ALU.subtract).then_inc(rope_r, 1)
                elif kind == "qkT":
                    c = rest[0]
                    taken(eng, ("eT", i))
                    landed(eng, work)
                    src = ps.rearrange("p (h t) -> p h t", h=4)
                    e = eT[:, int(c == "k"), :].unsqueeze(1).to_broadcast([P, 4, P])
                    dst = kT[:, :, i * P:(i + 1) * P] if c == "k" else qT[:, 4 * c:4 * c + 4, :]
                    tt(dst, src, e, ALU.add).then_inc(is_drained(work), 1)
                elif kind == "wo":
                    landed(eng, work)
                    if i:
                        eng.wait_ge(x_out, i)
                    tt(xtmp[:, :], ps[:, 0:D], g_row[:, 1, 0:D], ALU.mult).then_inc(is_drained(work), 1)
                    taken(eng, work)
                    tt(x[:, i, :], x[:, i, :], xtmp[:, :], ALU.add).then_inc(x_att, 1)
                elif kind == "gu":
                    c = rest[0]
                    cols = slice(c // 2 * 512, (c // 2 + 1) * 512)
                    landed(eng, work)
                    if c % 2 == 0:
                        eng.wait_ge(gu_tanh, 2 * i + c // 2 + 1)
                        if i:
                            landed(eng, ("hsT", i - 1, 1))
                        stt(sg[:, cols], tb[:, cols], 1.0, ps, ALU.add, ALU.mult).then_inc(is_drained(work), 1)
                    else:
                        taken(eng, ("gu", i, c - 1))
                        tt(sg[:, cols], sg[:, cols], ps, ALU.mult).then_inc(is_drained(work), 1)
                elif kind == "sparse":
                    taken(eng, ("gu", i, 3))
                    if i:
                        landed(eng, ("down", i - 1))
                    mark(stt(tb[:, :], sg[:, :], -1.0, sg[:, :], ALU.mult, ALU.max))
                    own()
                    a4 = tb[:, :].rearrange("p (g a b) -> p g a b", a=2, b=2)
                    c01_23, c02_13 = cmp_h[:, 0:2, :], cmp_h[:, 2:4, :]
                    mark(tt(c01_23.rearrange("p c g -> p g c"), a4[:, :, :, 0], a4[:, :, :, 1], ALU.is_ge))
                    mark(tt(c02_13.rearrange("p c g -> p g c"), a4[:, :, 0, :], a4[:, :, 1, :], ALU.is_ge))
                    mark(tt(cmp_h[:, 4, :], a4[:, :, 0, 0], a4[:, :, 1, 1], ALU.is_ge))
                    mark(tt(cmp_h[:, 5, :], a4[:, :, 0, 1], a4[:, :, 1, 0], ALU.is_ge))
                    own()
                    c01, c23, c02, c13, c03, c12 = (cmp_h[:, n, :] for n in range(6))
                    h4 = sg[:, :].rearrange("p (g j) -> p g j", j=4)
                    sp_ = [spt_h[:, n, :] for n in range(4)]
                    mark(tt(sp_[0], c01, c02, ALU.add))
                    mark(tt(sp_[1], c12, c13, ALU.add))
                    mark(tt(sp_[2], c02, c12, ALU.add))
                    mark(tt(sp_[3], c03, c13, ALU.add))
                    own()
                    mark(tt(sp_[0], sp_[0], c03, ALU.add))
                    mark(tt(sp_[1], sp_[1], c01, ALU.subtract))
                    mark(tt(sp_[2], sp_[2], c23, ALU.subtract))
                    mark(tt(sp_[3], sp_[3], c23, ALU.add))
                    own()
                    for j, (op, at) in enumerate(((ALU.is_ge, 1.5), (ALU.is_ge, 0.5), (ALU.is_lt, 0.5), (ALU.is_lt, 1.5))):
                        last = stt(h4[:, :, j], sp_[j], at, h4[:, :, j], op, ALU.mult)
                    last.then_inc(sparse_ready, 1)
                elif kind == "down":
                    landed(eng, work)
                    eng.wait_ge(x_att, i + 1)
                    stt(xtmp[:, :], ps[:, 0:D], 0.5, g_row[:, 1, D:2 * D], ALU.mult, ALU.mult).then_inc(is_drained(work), 1)
                    taken(eng, work)
                    tt(x[:, i, :], x[:, i, :], xtmp[:, :], ALU.add).then_inc(x_out, 1)

            for att, beside in steps:
                if att == (0, 0):
                    for h in range(AHEAD):
                        row_max(0, h)
                if att:
                    i, h = att
                    no = i * HQ + h
                    g = h // 4
                    if i >= 4:
                        n_pt = pt_no[i, h, 1]
                        landed(eng, ("O", *pt_key[n_pt - 2][:2]))
                        n = len(groups(i)[1]) * P
                        landed(eng, ("PT", i, h, 1))
                        nc.vector.tensor_copy(PT[:, n_pt % 2, 0:n], bank(("PT", i, h, 1))[:, 0:n]).then_inc(is_drained(("PT", i, h, 1)), 1)
                if att and after(att):
                    row_max(*after(att))
                for work in beside:
                    beside_dve(work)
                if att:
                    taken(eng, ("S", i, h))
                    mark(nc.vector.reciprocal(rinv[:, no % 4:no % 4 + 1], rsum[:, no % 4:no % 4 + 1]))
                    own()
                    eng.wait_ge(gate_ready, 4 * i + g + 1)
                    if h % 4 == 0 and 4 * i + g:
                        landed(eng, ("oT", *divmod(4 * i + g - 1, 4)))
                    landed(eng, ("O", i, h))
                    col = slice(h % 4 * P, (h % 4 + 1) * P)
                    stt(osb[:, col], bank(("O", i, h))[:, 0:DH], rinv[:, no % 4:no % 4 + 1],
                        gate[:, g % 2, col], ALU.mult, ALU.mult).then_inc(is_drained(("O", i, h)), 1)

        @block.gpsimd
        def _(eng):
            marks = [0]

            def mark(ins):
                marks[0] += 1
                ins.then_inc(pool, 1)

            def own():
                eng.wait_ge(pool, marks[0])

            ts, tt = nc.gpsimd.tensor_scalar, nc.gpsimd.tensor_tensor
            nc.gpsimd.memset(W1[:, :, :, H:HP], 0.0)
            nc.gpsimd.memset(W3[:, :, :, H:HP], 0.0)
            nc.gpsimd.memset(sw1[:, :, H:HP], 0.0)
            nc.gpsimd.memset(S[0:NS, 0], 0.0)
            mark(nc.gpsimd.memset(sw3[:, :, H:HP], 0.0))
            own()
            mark(nc.gpsimd.memset(sw2[H - 2 * P:P, 2, :], 0.0))
            own()
            nc.gpsimd.memset(xc[:, :, 0:3], 0.0).then_inc(pool_init, 1)

            def inv_sqrt(out, in_, tmp, mul, eps, n):
                mark(ts(tmp, in_, mul, eps, ALU.mult, ALU.add))
                own()
                return tt(out, tmp, half_neg[:, 0:n], ALU.pow)

            def scale_ln(n):
                s = n % 4
                eng.wait_ge(ln_stats, n + 1)
                inv_sqrt(ln_rstd[:, s:s + 1], ln_mv[:, s, 1:2], ln_t[:, s:s + 1], 1.0, 1e-5, 1).then_inc(ln_scaled, 1)

            eng.wait_ge(dve_init, 1)
            for i in range(NT):
                scale_ln(i)

            def over_p(t):
                return t.unsqueeze(2).to_broadcast([P, NH, P])

            def front(c):
                b = c % 2
                if c >= 2:
                    landed(eng, ("seg", c - 2))
                tt(M1[:, b], stril.unsqueeze(1).to_broadcast([P, NH, P]), over_p(a_dt(c)), ALU.mult).then_inc(m1_ready, 1)
                taken(eng, ("xtok", c))
                if c >= 2:
                    taken(eng, ("ydiag", c - 2))
                    eng.wait_ge(xs_ready, c - 1)
                tt(xD[:, b], x_sb, over_p(d_skip), ALU.mult).then_inc(xdt_ready, 1)
                tt(Xdt[:, b], x_sb, over_p(dtb[:, 9, c * NH:(c + 1) * NH]), ALU.mult).then_inc(xdt_ready, 1)

            eng.wait_ge(dt_ready, 1)
            front(0)
            for c in range(NT):
                if c + 1 < NT:
                    front(c + 1)
                if c:
                    eng.wait_ge(yg_sq, c)
                    landed(eng, ("ygT", c - 1))
                taken(eng, ("yoff", c))
                taken(eng, ("z", c))
                tt(yg, y1, zs[:, c, :].rearrange("p (h d) -> p h d", h=NH), ALU.mult).then_inc(yg_ready, 1)
                eng.wait_ge(yg_sq, c + 1)
                inv_sqrt(small[:, 24 + c:25 + c], small[:, 8 + c:9 + c], ln_t[:, 0:1], 1.0 / DI, 1e-5, 1).then_inc(yg_rstd, 1)
            eng.wait_ge(x_mixed, NT)
            nc.gpsimd.memset(small[:, 41:42], 0.0).then_inc(moe_free, 1)
            eng.wait_ge(moe_free, 2)
            nc.gpsimd.memset(W2[H - 2 * P:P, :, 2, :], 0.0).then_inc(pool_init, 1)
            eng.wait_ge(pool_init, 2)

            for i in range(NT):
                scale_ln(NT + i)
            eng.wait_ge(route_done, 1)
            eng.wait_ge(ln_done, 2 * NT)
            eng.wait_ge(zeroed, 16)
            for i in range(NT):
                nc.gpsimd.indirect_dma_start(
                    out=xd_d, out_offset=bass.IndirectOffsetOnAxis(ap=slot_u[:, 0, i:i + 1], axis=0),
                    in_=xn[:, i, :], in_offset=None, bounds_check=E * CAP - 1, oob_is_err=False).then_inc(scattered, 16)
            eng.wait_ge(oe_stored, 16 * E)
            landed(eng, ("xdT", 3))
            for i in range(NT):
                nc.gpsimd.indirect_dma_start(
                    out=og[:, i, :], out_offset=None, in_=oe_d,
                    in_offset=bass.IndirectOffsetOnAxis(ap=slot_u[:, 1, i:i + 1], axis=0),
                    bounds_check=E * CAP - 1, oob_is_err=False).then_inc(gathered, 16)
            eng.wait_ge(x_moe, NT)

            eng.wait_ge(loaded["tables"], 16)
            mark(ts(ln_w[:, :, 0, :], ln_w[:, :, 0, :], DH ** -0.5, 0.0, ALU.mult, ALU.add))
            mark(ts(ln_b[:, :, 0, :], ln_b[:, :, 0, :], DH ** -0.5, 0.0, ALU.mult, ALU.add))
            own()

            def rope_tables(i):
                cos, sin = (rope_cs[:, a, i, :].unsqueeze(1).to_broadcast([P, 2, 64]) for a in range(2))
                if i:
                    eng.wait_ge(rope_r, rope_no[i - 1, 3] + 1)
                    eng.wait_ge(rope_i, rope_no[i - 1, 3] + 1)
                    landed(eng, ("eT", i - 1))
                for s, (w, cs) in enumerate(((0, cos), (1, sin), (0, sin), (1, cos))):
                    mark(tt(rt[:, s], ln_w[:, w], cs, ALU.mult))
                t = rtmp.rearrange("p (s qk d) -> p s qk d", s=2, qk=2)
                for half, (c0, c1, op) in enumerate(((cos, sin, ALU.subtract), (sin, cos, ALU.add))):
                    mark(tt(t[:, 0], ln_b[:, 0], c0, ALU.mult))
                    mark(tt(t[:, 1], ln_b[:, 1], c1, ALU.mult))
                    own()
                    ins = tt(rope_E[:, :, half * 64:(half + 1) * 64], t[:, 0], t[:, 1], op)
                    if half:
                        ins.then_inc(tab_ready, 1)
                    else:
                        mark(ins)
                        own()

            def beside_pool(work):
                kind, i, *rest = work
                if kind in ("ln3", "ln4"):
                    scale_ln(ln_no[kind, i])
                    if kind == "ln3":
                        rope_tables(i)
                elif kind == "proj" and rest[0] != "v":
                    r_no = rope_no[i, rest[0]]
                    b = r_no % 2
                    eng.wait_ge(q_stats, r_no + 1)
                    inv_sqrt(q_rs[:, b, :], q_mv[:, b, :, 1], q_tt[:, b, :], 1.0, 1e-6, 4).then_inc(q_rstd, 1)
                elif kind == "rope":
                    r_no = rope_no[i, rest[0]]
                    b, qk = r_no % 2, int(rest[0] == "k")
                    eng.wait_ge(q_norm, r_no + 1)
                    if r_no:
                        eng.wait_ge(rope_i, r_no)
                    table = lambda s: rt[:, s, qk, :].unsqueeze(1).to_broadcast([P, 4, 64])
                    mark(tt(t_i[:, 0], raw_of(r_no)[:, :, 0:64], table(2), ALU.mult))
                    mark(tt(t_i[:, 1], raw_of(r_no)[:, :, 64:128], table(3), ALU.mult))
                    own()
                    if r_no > 4:
                        pi, pc = divmod(r_no - 1, 5)
                        landed(eng, ("qkT", pi, ("k", 0, 1, 2, 3)[pc]))
                    tt(roped_of(r_no)[:, :, 64:128], t_i[:, 0], t_i[:, 1], ALU.add).then_inc(rope_i, 1)
                elif kind == "gate":
                    no = 4 * i + rest[0]
                    taken(eng, work)
                    ts(gate[:, no % 2, :], gate[:, no % 2, :], 0.5, 0.5, ALU.mult, ALU.add).then_inc(gate_ready, 1)

            for att, beside in steps:
                for work in beside:
                    beside_pool(work)


def shape_constants():
    k = np.arange(P)
    ident = np.eye(P, dtype=np.float32)
    tri = (k[:, None] <= k[None, :]).astype(np.float32)
    stril = (k[:, None] > k[None, :]).astype(np.float32)
    rank_weight = np.tile(np.arange(E, 0, -1), NT)[None].repeat(P, 0).astype(np.float32)
    base = np.tile(np.arange(E) * CAP, NT)[None].repeat(P, 0).astype(np.float32)
    consts = np.concatenate([ident, tri, stril, rank_weight, base], axis=1)
    inv = np.float32(1.0) / np.float32(1000000.0) ** (np.arange(0, DH, 2, dtype=np.float32) / np.float32(DH))
    freqs = np.outer(np.arange(T, dtype=np.float32), inv.astype(np.float32)).astype(np.float32)
    cs = np.stack([np.cos(freqs), np.sin(freqs)]).astype(np.float32)
    tables = cs.reshape(2, NT, P, 64).transpose(2, 0, 1, 3).reshape(P, -1)
    return np.ascontiguousarray(consts), np.ascontiguousarray(tables)


def kernel(**inputs):
    import numpy as np
    import concourse.bacc as bacc
    from concourse import mybir
    from concourse.bass_utils import run_bass_kernel_spmd as run

    a = {name: np.asarray(value) for name, value in inputs.items()}
    consts, tables = shape_constants()
    cols = lambda t, n: t.reshape(n, P).T
    rows = lambda t: np.broadcast_to(t.reshape(1, -1), (P, t.size))
    even_odd = np.concatenate([np.arange(0, DH, 2), np.arange(1, DH, 2)])
    conv_w = a["L0_attn_conv_w"].reshape(5, P, 4).transpose(1, 0, 2).reshape(P, 20)
    norm = lambda kind: [rows(np.concatenate([a[f"L1_attn_{q}_norm_{kind}"][even_odd[ri * 64:ri * 64 + 64]]
                                              for ri in range(2) for q in "qk"]))]
    vectors = np.concatenate(
        [cols(a["L0_c"].reshape(-1), 2), cols(a["L1_c"].reshape(-1), 2), rows(a["L0_attn_dt_bias"]),
         rows(a["L0_attn_A_log"]), rows(a["L0_attn_D"]), cols(a["L0_attn_norm_w"], 4), conv_w,
         cols(a["L0_attn_conv_b"], 5), np.zeros((P, 3), np.float32)] + norm("w") + norm("b"), axis=1)
    wqkv = a["L1_attn_w_qkv"].reshape(5120 // DH, DH, D)
    perm = np.concatenate([wqkv[0:HQ][:, even_odd], wqkv[HQ:2 * HQ],
                           wqkv[2 * HQ:2 * HQ + HKV][:, even_odd], wqkv[2 * HQ + HKV:]])
    arrays = {
        "consts": consts, "tables": tables, "vectors": vectors, "x": a["L0_attn_u"],
        "W_in": a["L0_attn_W_in"], "W_out": a["L0_attn_W_out"], "Wg": a["L0_ffn_Wg"],
        "W1": a["L0_ffn_W1"], "W3": a["L0_ffn_W3"], "W2": a["L0_ffn_W2"], "sw1": a["L0_ffn_sw1"],
        "sw3": a["L0_ffn_sw3"], "sw2": a["L0_ffn_sw2"], "wmod0": a["L0_wmod"], "wmod1": a["L1_wmod"],
        "wqkv": perm.reshape(5120, D).T, "wo": a["L1_attn_w_o"].T, "wgate": a["L1_ffn_w_gate"],
        "wup": a["L1_ffn_w_up"], "wdown": a["L1_ffn_w_down"],
    }
    arrays = {f"in_{name}": np.ascontiguousarray(t) for name, t in arrays.items()}
    nc = bacc.Bacc("TRN2", target_bir_lowering=False, num_devices=1)
    args = [nc.dram_tensor(name, t.shape, mybir.dt.from_np(t.dtype), kind="ExternalInput").ap()
            for name, t in arrays.items()]
    out = nc.dram_tensor("out", (1, T, D), mybir.dt.float32, kind="ExternalOutput").ap()
    build(nc, *args, out)
    return run(nc, [arrays], core_ids=[0]).results[0]["out"]
```

```python
from contextlib import ExitStack

import concourse.bass as bass
import numpy as np
from concourse import mybir

ALU = mybir.AluOpType
ACT = mybir.ActivationFunctionType
F32 = mybir.dt.float32
BF16 = mybir.dt.bfloat16
F16 = mybir.dt.float16
U32 = mybir.dt.uint32
AX_X = mybir.AxisListType.X

P = 128
T = 1024
NT = T // P
D = 256
KD = D // P
DI = 512
NH = 4
NS = 64
E = 8
CAP = T // E
H = 352
KH = 3
HP = KH * P
HQ, HKV, DH = 16, 4, 128
REP = HQ // HKV
FF = 1024
MASKED = -1e30
NEVER = 4096.0


class PsumPlan:

    def __init__(self):
        self.turn = {}
        self.used = {}

    def add(self, job, slot):
        assert job not in self.turn, job
        self.turn[job] = (slot, self.used.get(slot, 0))
        self.used[slot] = self.used.get(slot, 0) + 1


MOE_HT_AT = {0: 5, 1: 7}


def layer0_jobs():
    jobs = [("modcol", 0)]
    jobs += [("hT", "mix", g) for g in range(NT // 2)]
    jobs += [("dt",)]
    for n in range(2):
        jobs += [("xbc", n, m) for m in range(5)]
        jobs += [("z", i) for i in range(4 * n, 4 * n + 4)]
    jobs += [("modcol", 1), ("modrow", 0), ("modrow", 1)]
    front = lambda c: [("xtok", c), ("misc", c), ("seg", c)]
    jobs += front(0)
    for c in range(NT):
        jobs += [("yoff", c), ("ydiag", c), ("state", c)]
        jobs += [("ygT", c - 1)] if c else []
        jobs += front(c + 1) if c + 1 < NT else []
        jobs += [("mixout", c - 1)] if c else []
        jobs += [("hT", "moe", g) for g, at in MOE_HT_AT.items() if at == c]
    jobs += [("ygT", NT - 1), ("mixout", NT - 1)]
    jobs += [("hT", "moe", g) for g in range(NT // 2) if g not in MOE_HT_AT]
    jobs += [("logits",)]
    for m in range(KH):
        jobs += [("sh1", 0, m), ("sh3", 0, m)]
        jobs += [("rank",)] if m == 0 else []
    jobs += [("shout", i) for i in range(4)]
    jobs += [("xdT", g) for g in range(4)]
    jobs += [("e1", 0), ("e3", 0)]
    for e in range(E):
        jobs += [("e1", e + 1), ("e3", e + 1)] if e + 1 < E else []
        jobs += [("eout", e)]
    return jobs


BESIDE = {
    0: [("ln3", 1), ("oT", -1, 3)],
    1: [("gate", 0, 1), ("h3T", 1), ("wo", -1)],
    2: [("ln4", -1), ("proj", 1, "k"), ("eT", 1)],
    3: [("proj", 1, "v"), ("rope", 1, "k"), ("h4T", -1)],
    4: [("proj", 1, 0), ("oT", 0, 0), ("qkT", 1, "k")],
    5: [("gate", 0, 2), ("split", 1, "k"), ("rope", 1, 0), ("gu", -1, 0)],
    6: [("proj", 1, 1), ("gu", -1, 1), ("qkT", 1, 0)],
    7: [("split", 1, 0), ("rope", 1, 1), ("gu", -1, 2)],
    8: [("gu", -1, 3), ("oT", 0, 1), ("qkT", 1, 1), ("sparse", -1, 0)],
    9: [("sparse", -1, 1), ("proj", 1, 2), ("split", 1, 1)],
    10: [("rope", 1, 2)],
    11: [("gate", 0, 3), ("sparse", -1, 2), ("qkT", 1, 2)],
    12: [("sparse", -1, 3), ("proj", 1, 3), ("oT", 0, 2), ("split", 1, 2)],
    13: [("rope", 1, 3)],
    14: [("gate", 1, 0), ("hsT", -1, 0), ("hsT", -1, 1), ("qkT", 1, 3)],
    15: [("split", 1, 3), ("down", -1)],
}


def layer1_steps():
    first = [("sh1", 1, 0), ("sh3", 1, 0), ("sh1", 1, 1), ("sh3", 1, 1), ("combine", 0), ("ln3", 0),
             ("sh1", 1, 2), ("sh3", 1, 2), ("combine", 1), ("h3T", 0), ("combine", 2), ("combine", 3),
             ("proj", 0, "k"), ("proj", 0, 0), ("proj", 0, "v"), ("eT", 0), ("rope", 0, "k"),
             ("proj", 0, 1), ("rope", 0, 0), ("qkT", 0, "k"), ("split", 0, "k"), ("proj", 0, 2),
             ("rope", 0, 1), ("qkT", 0, 0), ("proj", 0, 3), ("split", 0, 0), ("rope", 0, 2), ("qkT", 0, 1),
             ("gate", 0, 0), ("split", 0, 1), ("rope", 0, 3), ("qkT", 0, 2), ("split", 0, 2),
             ("qkT", 0, 3), ("split", 0, 3)]
    late = {h: [("shout", 4 + h // 2 - 1), ("combine", 4 + h // 2 - 1)] for h in (2, 4, 6, 8)}
    last = [("oT", 3), ("wo",), ("ln4",), ("h4T",), ("gu", 0), ("gu", 1), ("gu", 2), ("gu", 3),
            ("sparse", 0), ("sparse", 1), ("sparse", 2), ("sparse", 3), ("hsT", 0), ("hsT", 1), ("down",)]
    steps = [(None, [work]) for work in first]
    for i in range(NT):
        for h in range(HQ):
            beside = [(kind, i + di, *rest) for kind, di, *rest in BESIDE[h] if 0 <= i + di < NT]
            steps.append(((i, h), beside + (late.get(h, []) if i == 0 else [])))
    return steps + [(None, [(kind, NT - 1, *rest)]) for kind, *rest in last]


AHEAD = 2


def after(att):
    i, h = att
    n = i * HQ + h + AHEAD
    return (n // HQ, n % HQ) if n < NT * HQ else None


def groups(i):
    return [range(j, min(j + 4, i + 1)) for j in range(0, i + 1, 4)]


W_SCALE = 2.0 ** 10
Q_SCALE, K_SCALE = 2.0 ** 7, 2.0 ** 4
S_UNSCALE = 1.0 / (Q_SCALE * K_SCALE)
PAIRS = ((0, 0), (1, 0), (0, 1))
W_ORDER = (8, 0, 9, 1, 2, 3, 4, 5, 6, 7)
W_PARTS = 2 * len(W_ORDER)

PSUM_OF = {"proj": "M", "gate": "M", "wo": "M", "gu": "M", "down": "M",
           "sh1": "M", "sh3": "M", "shout": "M",
           "h3T": "T", "h4T": "T", "eT": "T", "qkT": "T", "oT": "T", "hsT": "T"}


def layer1_jobs(steps):
    jobs = []
    turns = big = 0
    for att, beside in steps:
        if att == (0, 0):
            jobs += [(("S", 0, h), f"S{h % 2}") for h in range(AHEAD)]
        if att:
            for g in range(len(groups(att[0]))):
                jobs.append((("PT", *att, g), f"T{turns % 2}"))
                turns += 1
        if att and after(att):
            i, h = after(att)
            jobs.append((("S", i, h), f"S{h % 2}"))
        for work in beside:
            if work[0] in PSUM_OF:
                slot = PSUM_OF[work[0]]
                if slot == "T":
                    slot = f"T{turns % 2}"
                    turns += 1
                elif att is None:
                    slot = ("M", "O", "S0", "S1")[big % 4]
                    big += 1
                jobs.append((work, slot))
        if att:
            jobs.append((("O", *att), "O"))
    return jobs


def build(nc, consts_d, tables_d, vectors_d, x_d, W_in_d, W_out_d, Wg_d, W1_d, W3_d, W2_d, sw1_d,
          sw3_d, sw2_d, wmod0_d, wmod1_d, wqkv_d, wo_d, wgate_d, wup_d, wdown_d, out_d):
    xd_d = nc.dram_tensor("expert_rows", [E * CAP, D], F32, kind="Internal").ap()
    oe_d = nc.dram_tensor("expert_outputs", [E * CAP, D], F32, kind="Internal").ap()
    ctx = ExitStack()
    with ctx:
        def sb(name, words, dt=F32, parts=P):
            return ctx.enter_context(nc.sbuf_tensor(name, [parts, words], dt))

        def sem(name):
            return ctx.enter_context(nc.semaphore(name))

        consts = sb("consts", 512)
        ident, tri, stril = (consts[:, k * P:(k + 1) * P] for k in range(3))
        rank_weight, expert_base = consts[:, 384:448], consts[:, 448:512]
        rope_cos_sin = sb("rope_cos_sin", 2 * NT * 64)
        rope_cs = rope_cos_sin[:, :].rearrange("p (a i d) -> p a i d", a=2, i=NT)
        x = sb("x", NT * D)[:, :].rearrange("p (i d) -> p i d", i=NT)
        vectors = sb("vectors", 560)
        c_cols = vectors[:, 0:4]
        dt_bias, a_log, d_skip = vectors[:, 4:8], vectors[:, 8:12], vectors[:, 12:16]
        norm_w = vectors[:, 16:20]
        conv_w = vectors[:, 20:40].rearrange("p (m j) -> p m j", m=5)
        conv_b = vectors[:, 40:45]
        ln_w = vectors[:, 48:304].rearrange("p (ri qk d) -> p ri qk d", ri=2, qk=2)
        ln_b = vectors[:, 304:560].rearrange("p (ri qk d) -> p ri qk d", ri=2, qk=2)
        ones = sb("ones", P)
        ident_h = sb("ident_h", P, BF16)
        mask_h = sb("mask_h", P, BF16)
        mod_col = sb("mod_col", 16)
        g_row = sb("g_row", 2 * 512)[:, :].rearrange("p (l n) -> p l n", l=2)
        ln_st = sb("ln_st", 4 * 6)[:, :].rearrange("p (s n) -> p s n", s=4)
        ln_mv = sb("ln_mv", 4 * 2)[:, :].rearrange("p (s n) -> p s n", s=4)
        ln_rstd = sb("ln_rstd", 4)
        ln_t = sb("ln_t", 4)
        half_neg = sb("half_neg", 4)
        xtmp = sb("xtmp", D)
        route = sb("route", 5 * 64)[:, :].rearrange("p (s n) -> p s n", s=5)
        rt8 = sb("rt8", 9 * 8)[:, :].rearrange("p (s n) -> p s n", s=9)
        slot_u = sb("slot_u", 2 * 8, U32)[:, :].rearrange("p (s n) -> p s n", s=2)
        dtb = sb("dtb", 12 * 32)[:, :].rearrange("p (s n) -> p s n", s=12)
        small = sb("small", 64)
        a_dt = lambda c: dtb[:, 10, c * NH:(c + 1) * NH]
        dt_as_relu = dtb[:, 11, :]

        words = (nc.sbuf_usable_end - nc.sbuf_base) // 4 - 40
        arena = sb("arena", words)

        class Region:
            def __init__(self, at, end):
                self.at, self.end = at, end

            def take(self, n):
                a = arena[:, self.at:self.at + n]
                self.at += n
                assert self.at <= self.end, (self.at, self.end)
                return a

        TAIL = 2 * E * KD * HP + 3 * KH * D
        moe_at = words - TAIL
        r = Region(moe_at, words)
        W1 = r.take(E * KD * HP).rearrange("p (e k h) -> p e k h", e=E, k=KD)
        W3 = r.take(E * KD * HP).rearrange("p (e k h) -> p e k h", e=E, k=KD)
        sw1 = r.take(KD * HP).rearrange("p (k h) -> p k h", k=KD)
        sw3 = r.take(KD * HP).rearrange("p (k h) -> p k h", k=KD)
        sw2 = r.take(KH * D).rearrange("p (k n) -> p k n", k=KH)
        r = Region(0, moe_at)
        xn = r.take(NT * D).rearrange("p (i d) -> p i d", i=NT)
        hT = r.take(KD * T).rearrange("p (n k t) -> p n k t", n=2, k=KD)
        hT_of = lambda k, i: hT[:, i // 4, k, i % 4 * P:(i % 4 + 1) * P]
        Wg = r.take(KD * E).rearrange("p (k e) -> p k e", k=KD)
        moe_acts = r.at
        W_in = r.take(KD * 1156).rearrange("p (k n) -> p k n", k=KD)
        W_out = r.take(4 * D).rearrange("p (k n) -> p k n", k=4)
        xc = r.take(5 * (T + 3)).rearrange("p (m t) -> p m t", m=5)
        xT = r.take(5 * T).rearrange("p (m t) -> p m t", m=5)
        BT = xT[:, 4, :]
        CT = r.take(T)
        zs = r.take(NT * DI).rearrange("p (i n) -> p i n", i=NT)
        two = lambda n: r.take(2 * n).rearrange("p (b n) -> p b n", b=2)
        Xdt, xD, M1, MT, Xs, S = (two(DI).rearrange("p b (h d) -> p b h d", h=NH) for _ in range(6))
        Lm = r.take(DI).rearrange("p (h d) -> p h d", h=NH)
        Gm = r.take(P)
        y1, ygT = (r.take(DI).rearrange("p (h d) -> p h d", h=NH) for _ in range(2))
        B_tok = two(NS)
        es = two(8)
        sq_out = xc[:, 0, 0:DI]
        yg, x_sb = (xc[:, m, 0:2 * DI].rearrange("p (b h d) -> p b h d", b=2, h=NH) for m in (1, 2))
        zeros = ygT[:, 0:2, :].rearrange("p a b -> p (a b)")
        r = Region(moe_at, words)
        wmod = r.take(2 * KD * 1536).rearrange("p (l k n) -> p l k n", l=2, k=KD)
        sc_b = r.take(4 * P).rearrange("p (s n) -> p s n", s=4)
        g_abs = r.take(512)
        r = Region(moe_acts, moe_at)
        wqkv = r.take(KD * 5120).bitcast(F16).rearrange("p (c v k n) -> p c v k n", c=10, v=2, k=KD)
        l1_acts = r.at
        W2 = r.take(E * KH * D).rearrange("p (e k n) -> p e k n", e=E, k=KH)
        og = r.take(E * D).rearrange("p (e d) -> p e d", e=E)
        hs_0 = r.take(KH * 512)
        s1 = r.take(2 * 512).rearrange("p (b n) -> p b n", b=2)
        xd = r.take(E * D).rearrange("p (e d) -> p e d", e=E)
        xdT = r.take(KD * E * P).rearrange("p (k e s) -> p k e s", k=KD, e=E)
        se = r.take(2 * HP).rearrange("p (b n) -> p b n", b=2)
        he = r.take(2 * HP).rearrange("p (b n) -> p b n", b=2)
        oe = xn
        r = Region(moe_at, words)
        wo = r.take(HQ * D).rearrange("p (h n) -> p h n", h=HQ)
        wgate = r.take(KD * FF).rearrange("p (k n) -> p k n", k=KD)
        wup = r.take(KD * FF).rearrange("p (k n) -> p k n", k=KD)
        wdown = r.take(FF // P * D).rearrange("p (k n) -> p k n", k=FF // P)
        sg = r.take(FF)
        tb = r.take(FF)
        hs_1 = arena[:, r.at - 2 * FF:r.at - 2 * FF + KH * 512]
        hsT = r.take(FF).rearrange("p (k t) -> p k t", k=FF // P)
        spt_h = hsT[:, 0:4, :].rearrange("p k t -> p (k t)").bitcast(BF16).rearrange("p (n g) -> p n g", n=4)
        h4T = r.take(D).rearrange("p (k t) -> p k t", k=KD)
        cmp_h = r.take(6 * P).bitcast(BF16).rearrange("p (c g) -> p c g", c=6)
        r = Region(l1_acts, moe_at)
        kT = r.take(HKV * T).bitcast(F16).rearrange("p (v h t) -> p v h t", v=2, h=HKV)
        v = r.take(NT * HKV * DH).rearrange("p (i n) -> p i n", i=NT)
        qT = r.take(HQ * P).bitcast(F16).rearrange("p (v h t) -> p v h t", v=2, h=HQ)
        pr = two(T)
        oT = r.take(HQ * P).rearrange("p (h t) -> p h t", h=HQ)
        PT = two(512)
        gate = two(512)
        raw_words, roped_words = (r.take(512) for _ in range(2))
        raw, roped = (t.rearrange("p (h d) -> p h d", h=4) for t in (raw_words, roped_words))
        og_words = og.rearrange("p e d -> p (e d)")
        staged = [raw_words, roped_words, og_words[:, 0:512], og_words[:, 512:1024]]
        hs = [t.rearrange("p (k t) -> p k t", k=KH) for t in (hs_0, hs_1)]
        s1_of = lambda n, m: (s1[:, 0], s1[:, 1], PT[:, 1], tb[:, 512:1024])[2 * n + (KH * n + m) % 2]
        r = Region(0, moe_acts)
        raws = [oT[:, 4 * n:4 * n + 4, :] for n in range(4)]
        ropeds = [pr[:, n // 2, n % 2 * 512:(n % 2 + 1) * 512].rearrange("p (h d) -> p h d", h=4) for n in range(4)]
        raw_of = lambda r_no: raws[r_no] if r_no < 4 else raw
        roped_of = lambda r_no: ropeds[r_no] if r_no < 4 else roped
        xn1, h3T = [r.take(D)], [r.take(D)]
        rt = r.take(4 * 128).rearrange("p (s qk d) -> p s qk d", s=4, qk=2)
        t_r = r.take(512).rearrange("p (s h d) -> p s h d", s=2, h=4)
        t_i = r.take(512).rearrange("p (s h d) -> p s h d", s=2, h=4)
        assert r.at == NT * D
        rope_E = r.take(256).rearrange("p (qk d) -> p qk d", qk=2)
        eT = r.take(256).rearrange("p (qk t) -> p qk t", qk=2)
        rtmp = r.take(256)
        q_st = r.take(2 * 4 * 6).rearrange("p (b h n) -> p b h n", b=2, h=4)
        q_mv = r.take(2 * 4 * 2).rearrange("p (b h n) -> p b h n", b=2, h=4)
        q_rs = two(4)
        q_tt = two(4)
        nmax, rsum, rinv = r.take(4), r.take(4), r.take(4)
        r = Region(NT * D + KD * 512, moe_acts)
        osb = r.take(512)
        xn1.append(r.take(D))
        h3T.append(r.take(D))
        h3T = [t.bitcast(F16).rearrange("p (v k t) -> p v k t", v=2, k=KD) for t in h3T]
        h3_full = consts[:, 256:512].rearrange("p (k t) -> p k t", k=KD)
        sum_of = lambda r_no: raws[r_no] if r_no < 4 else roped
        nmax_scaled = small[:, 42:46]

        def qk_of(work):
            _, i, c = work
            if c == "k":
                return lambda v: kT[:, v, :, i * P:(i + 1) * P]
            return lambda v: qT[:, v, 4 * c:4 * c + 4, :]

        psum = ctx.enter_context(nc.psum_tensor("psum", [P, 8, 512], F32))

        steps = layer1_steps()
        plan = PsumPlan()
        for n, job in enumerate(layer0_jobs()):
            plan.add(job, n % 8)
        for job, slot in layer1_jobs(steps):
            plan.add(job, slot)
        BANK_OF = {"S0": 0, "S1": 2, "T0": 4, "T1": 5, "O": 6, "M": 7}
        filled = {s: sem(f"filled_{s}") for s in plan.used}
        drained = {s: sem(f"drained_{s}") for s in plan.used}

        def bank(job):
            slot = plan.turn[job][0]
            b = BANK_OF.get(slot, slot)
            if job[0] == "S":
                return psum[:, b:b + 2, :].rearrange("p b n -> p (b n)")
            return psum[:, b, :]

        def landed(eng, job):
            slot, n = plan.turn[job]
            eng.wait_ge(filled[slot], n + 1)

        def taken(eng, job):
            slot, n = plan.turn[job]
            eng.wait_ge(drained[slot], n + 1)

        def is_drained(job):
            return drained[plan.turn[job][0]]

        def is_filled(job):
            return filled[plan.turn[job][0]]

        ln_order = [("mix", i) for i in range(NT)] + [("moe", i) for i in range(NT)]
        for _, beside in steps:
            ln_order += [(w[0], w[1]) for w in beside if w[0] in ("ln3", "ln4")]
        ln_no = {key: n for n, key in enumerate(ln_order)}
        sparse_no = lambda i: i + 1
        rope_no = {}
        for i in range(NT):
            for c in ("k", 0, 1, 2, 3):
                rope_no[i, c] = len(rope_no)
        pt_no = {}
        for i in range(NT):
            for h in range(HQ):
                for g in range(len(groups(i))):
                    pt_no[i, h, g] = len(pt_no)
        pt_key = {n: key for key, n in pt_no.items()}

        names = ["consts", "tables", "vectors", "x", "W_in", "W_out", "Wg", "W1", "W3", "W2",
                 "sw", "wmod0", "wmod1", "wo", "wffn", "xd_rows"]
        loaded = {n: sem(f"loaded_{n}") for n in names}
        pads = sem("pads")
        zeroed = sem("zeroed")
        scattered = sem("scattered")
        oe_stored = sem("oe_stored")
        gathered = [sem(f"gathered_{i}") for i in range(NT)]
        stored = sem("stored")
        pool_init = sem("pool_init")
        dve_init = sem("dve_init")
        sc_ready = sem("sc_ready")
        scb_ready = sem("scb_ready")
        g_ready = sem("g_ready")
        dve = sem("dve")
        act = sem("act")
        pool = sem("pool")
        ln_stats, ln_scaled, ln_done = sem("ln_stats"), sem("ln_scaled"), sem("ln_done")
        conv_in, conv_done, conv_silu = sem("conv_in"), sem("conv_done"), sem("conv_silu")
        dt_abs, dt_exp, a_exp, dt_ready = sem("dt_abs"), sem("dt_exp"), sem("a_exp"), sem("dt_ready")
        m1_ready, misc_act, xdt_ready = sem("m1_ready"), sem("misc_act"), sem("xdt_ready")
        mt_ready, xs_ready, y_ready = sem("mt_ready"), sem("xs_ready"), sem("y_ready")
        yg_ready, yg_sq, yg_rstd = sem("yg_ready"), sem("yg_sq"), sem("yg_rstd")
        x_mixed = sem("x_mixed")
        moe_free = sem("moe_free")
        route_d, route_e, oh_ready, route_done = (sem("route_d"), sem("route_e"), sem("oh_ready"),
                                                  sem("route_done"))
        s1_ready, se_ready = sem("s1_ready"), sem("se_ready")
        x_shared, x_moe = sem("x_shared"), sem("x_moe")
        tab_ready, q_stats, q_rstd, q_norm = (sem("tab_ready"), sem("q_stats"), sem("q_rstd"),
                                              sem("q_norm"))
        rope_r, rope_i = sem("rope_r"), sem("rope_i")
        maxed, max_scaled = sem("maxed"), sem("max_scaled")
        w_full, w_hi, w_split = [sem(f"w_full_{b}") for b in range(4)], sem("w_hi"), sem("w_split")
        h3_split, qk_hi, qk_split = sem("h3_split"), sem("qk_hi"), sem("qk_split")
        gate_tanh, gate_ready = sem("gate_tanh"), sem("gate_ready")
        x_att, x_out = sem("x_att"), sem("x_out")
        gu_tanh, sparse_ready = sem("gu_tanh"), sem("sparse_ready")

        block = ctx.enter_context(nc.Block())

        @block.sync
        def _(sp):
            sp.dma_start(vectors[:, :], vectors_d).then_inc(loaded["vectors"], 16)
            sp.dma_start(x, x_d[0].rearrange("(i p) d -> p i d", p=P)).then_inc(loaded["x"], 16)
            sp.dma_start(consts[:, :], consts_d).then_inc(loaded["consts"], 16)
            sp.dma_start(wmod[:, 0], wmod0_d.rearrange("(k p) n -> p k n", p=P)).then_inc(loaded["wmod0"], 16)
            sp.dma_start(W_in, W_in_d.rearrange("(k p) n -> p k n", p=P)).then_inc(loaded["W_in"], 16)
            sp.dma_start(wmod[:, 1], wmod1_d.rearrange("(k p) n -> p k n", p=P)).then_inc(loaded["wmod1"], 16)
            sp.dma_start(W_out, W_out_d.rearrange("(k p) n -> p k n", p=P)).then_inc(loaded["W_out"], 16)
            sp.dma_start(Wg, Wg_d.rearrange("(k p) n -> p k n", p=P)).then_inc(loaded["Wg"], 16)
            sp.wait_ge(pool_init, 1)
            for w, w_d in ((sw1, sw1_d), (sw3, sw3_d)):
                sp.dma_start(w[:, :, 0:H], w_d.rearrange("(k p) h -> p k h", p=P)).then_inc(loaded["sw"], 16)
            sp.dma_start(sw2[:, 0:2, :], sw2_d[0:2 * P].rearrange("(k p) n -> p k n", p=P)).then_inc(loaded["sw"], 16)
            sp.dma_start(sw2[0:H - 2 * P, 2, :], sw2_d[2 * P:H]).then_inc(loaded["sw"], 16)
            sp.wait_ge(dve_init, 1)
            sp.dma_start(xd_d.rearrange("(e s) d -> s e d", e=E),
                         zeros.unsqueeze(1).to_broadcast([P, E, D])).then_inc(zeroed, 16)
            sp.dma_start(rope_cos_sin[:, :], tables_d).then_inc(loaded["tables"], 16)
            sp.wait_ge(pads, 1)
            for e in range(E):
                sp.dma_start(W1[:, e, :, 0:H], W1_d[e].rearrange("(k p) h -> p k h", p=P)).then_inc(loaded["W1"], 16)
                sp.dma_start(W3[:, e, :, 0:H], W3_d[e].rearrange("(k p) h -> p k h", p=P)).then_inc(loaded["W3"], 16)
            sp.wait_ge(x_mixed, NT)
            sp.wait_ge(moe_free, 2)
            sp.wait_ge(pool_init, 2)
            for e in range(E):
                sp.dma_start(W2[:, e, 0:2, :], W2_d[e, 0:2 * P].rearrange("(k p) n -> p k n", p=P)).then_inc(loaded["W2"], 16)
                sp.dma_start(W2[0:H - 2 * P, e, 2, :], W2_d[e, 2 * P:H]).then_inc(loaded["W2"], 16)

            def load_w(n):
                if n >= 4:
                    sp.wait_ge(w_split, n - 3)
                cols = slice(W_ORDER[n // 2] * 512, (W_ORDER[n // 2] + 1) * 512)
                sp.dma_start(staged[n % 4], wqkv_d[n % 2 * P:(n % 2 + 1) * P, cols]).then_inc(w_full[n % 4], 16)

            for n in range(4):
                load_w(n)
            sp.wait_ge(scattered, 16 * NT)
            sp.dma_start(xd, xd_d.rearrange("(e s) d -> s e d", e=E)).then_inc(loaded["xd_rows"], 16)
            for n in range(4, W_PARTS):
                load_w(n)
            for i in range(NT):
                sp.wait_ge(gathered[i], 16)
            landed(sp, ("eout", E - 1))
            sp.dma_start(wo, wo_d.rearrange("(h p) n -> p h n", p=P)).then_inc(loaded["wo"], 16)
            sp.dma_start(wgate, wgate_d.rearrange("(k p) n -> p k n", p=P)).then_inc(loaded["wffn"], 16)
            sp.dma_start(wup, wup_d.rearrange("(k p) n -> p k n", p=P)).then_inc(loaded["wffn"], 16)
            sp.dma_start(wdown, wdown_d.rearrange("(k p) n -> p k n", p=P)).then_inc(loaded["wffn"], 16)
            for i in range(NT):
                sp.wait_ge(x_out, i + 1)
                sp.dma_start(out_d[0, i * P:(i + 1) * P, :], x[:, i, :]).then_inc(stored, 16)
            sp.wait_ge(stored, 16 * NT)

        @block.tensor
        def _(pe):
            order = iter(plan.turn)

            def claim(job):
                assert next(order) == job, job
                slot, n = plan.turn[job]
                if n:
                    pe.wait_ge(drained[slot], n)
                return bank(job)

            def mm(out, lhsT, rhs, start=True, stop=True):
                return nc.tensor.matmul(out, lhsT=lhsT, rhs=rhs, start=start, stop=stop)

            def mod_columns(l):
                pe.wait_ge(loaded[f"wmod{l}"], 16)
                ps = claim(("modcol", l))
                for j, at in enumerate((0, 128, 256, 384, 768, 896, 1024, 1152)):
                    for k in range(KD):
                        last = mm(ps[:, j:j + 1], wmod[:, l, k, at:at + P],
                                  small[:, 2 * l + k:2 * l + k + 1], k == 0, k == KD - 1)
                last.then_inc(is_filled(("modcol", l)), 1)

            pe.wait_ge(sc_ready, 1)
            mod_columns(0)

            def transpose_h(which, g):
                pe.wait_ge(ln_done, ln_no[which, 2 * g + 1] + 1)
                ps = claim(("hT", which, g))
                for k in range(KD):
                    for t in range(2):
                        last = nc.tensor.transpose(ps[:, k * D + t * P:k * D + (t + 1) * P],
                                                   xn[:, 2 * g + t, k * P:(k + 1) * P], ident)
                last.then_inc(is_filled(("hT", which, g)), 1)

            for g in range(NT // 2):
                transpose_h("mix", g)

            pe.wait_ge(loaded["W_in"], 16)
            for g in range(NT // 2):
                taken(pe, ("hT", "mix", g))
            ps = claim(("dt",))
            for i in range(NT):
                for k in range(KD):
                    last = mm(ps[:, i * NH:(i + 1) * NH], hT_of(k, i),
                              W_in[:, k, 1152:1156], k == 0, k == KD - 1)
            last.then_inc(is_filled(("dt",)), 1)
            for n in range(2):
                for m in range(5):
                    ps = claim(("xbc", n, m))
                    for k in range(KD):
                        last = mm(ps, W_in[:, k, DI + m * P:DI + (m + 1) * P],
                                  hT[:, n, k, :], k == 0, k == KD - 1)
                    last.then_inc(is_filled(("xbc", n, m)), 1)
                for i in range(4 * n, 4 * n + 4):
                    ps = claim(("z", i))
                    for k in range(KD):
                        last = mm(ps, hT_of(k, i), W_in[:, k, 0:DI], k == 0, k == KD - 1)
                    last.then_inc(is_filled(("z", i)), 1)

            mod_columns(1)
            pe.wait_ge(scb_ready, 1)
            for l in range(2):
                ps = claim(("modrow", l))
                for j, at in enumerate((512, 1280)):
                    for k in range(KD):
                        last = mm(ps[:, j * D:(j + 1) * D], sc_b[:, 2 * l + k, :],
                                  wmod[:, l, k, at:at + D], k == 0, k == KD - 1)
                last.then_inc(is_filled(("modrow", l)), 1)

            def front(c):
                cols = slice(c * P, (c + 1) * P)
                pe.wait_ge(conv_silu, 5 * (c // 4) + 5)
                ps = claim(("xtok", c))
                for m in range(4):
                    last = nc.tensor.transpose(ps[:, m * P:(m + 1) * P], xT[:, m, cols], ident)
                last.then_inc(is_filled(("xtok", c)), 1)
                ps = claim(("misc", c))
                pe.wait_ge(dt_ready, 1)
                nc.tensor.transpose(ps[:, 0:NS], BT[0:NS, cols], ident[0:NS, 0:NS])
                mm(ps[:, P:2 * P], BT[0:NS, cols], CT[0:NS, cols])
                mm(ps[:, 256:260], tri, a_dt(c))
                mm(ps[:, 260:264], ones[:, :], a_dt(c)).then_inc(is_filled(("misc", c)), 1)
                ps = claim(("seg", c))
                pe.wait_ge(m1_ready, c + 1)
                for h in range(NH):
                    last = mm(ps[:, h * P:(h + 1) * P], M1[:, c % 2, h, :], tri)
                last.then_inc(is_filled(("seg", c)), 1)

            def turn_yg(c):
                ps = claim(("ygT", c))
                pe.wait_ge(yg_ready, c + 1)
                for m in range(4):
                    last = nc.tensor.transpose(ps[:, m * P:(m + 1) * P], yg[:, c % 2, m, :], ident)
                last.then_inc(is_filled(("ygT", c)), 1)

            def mix_out(c):
                ps = claim(("mixout", c))
                taken(pe, ("ygT", c))
                for k in range(4):
                    last = mm(ps[:, 0:D], ygT[:, k, :], W_out[:, k, :], k == 0, k == 3)
                last.then_inc(is_filled(("mixout", c)), 1)

            pe.wait_ge(loaded["W_out"], 16)
            front(0)
            for c in range(NT):
                cols = slice(c * P, (c + 1) * P)
                ps = claim(("yoff", c))
                if c:
                    taken(pe, ("state", c - 1))
                else:
                    pe.wait_ge(pool_init, 1)
                mm(ps, CT[0:NS, cols], S[0:NS, c % 2].rearrange("p h d -> p (h d)")).then_inc(is_filled(("yoff", c)), 1)
                ps = claim(("ydiag", c))
                pe.wait_ge(mt_ready, c + 1)
                pe.wait_ge(xdt_ready, 2 * c + 2)
                for h in range(NH):
                    last = mm(ps[:, h * P:(h + 1) * P], MT[:, c % 2, h, :], Xdt[:, c % 2, h, :])
                last.then_inc(is_filled(("ydiag", c)), 1)
                ps = claim(("state", c))
                pe.wait_ge(xs_ready, c + 1)
                pe.wait_ge(misc_act, c + 1)
                mm(ps[0:NS, :], B_tok[:, c % 2, :], Xs[:, c % 2].rearrange("p h d -> p (h d)")).then_inc(is_filled(("state", c)), 1)
                if c:
                    turn_yg(c - 1)
                if c + 1 < NT:
                    front(c + 1)
                if c:
                    mix_out(c - 1)
                for g, at in MOE_HT_AT.items():
                    if at == c:
                        transpose_h("moe", g)
            turn_yg(NT - 1)
            mix_out(NT - 1)

            for g in range(NT // 2):
                if g not in MOE_HT_AT:
                    transpose_h("moe", g)
            pe.wait_ge(loaded["Wg"], 16)
            for g in range(NT // 2):
                taken(pe, ("hT", "moe", g))
            ps = claim(("logits",))
            for i in range(NT):
                for k in range(KD):
                    last = mm(ps[:, i * E:(i + 1) * E], hT_of(k, i), Wg[:, k, :],
                              k == 0, k == KD - 1)
            last.then_inc(is_filled(("logits",)), 1)
            def shared_up(name, n, m):
                w = {"sh1": sw1, "sh3": sw3}[name]
                ps = claim((name, n, m))
                for k in range(KD):
                    last = mm(ps, w[:, k, m * P:(m + 1) * P], hT[:, n, k, :], k == 0, k == KD - 1)
                last.then_inc(is_filled((name, n, m)), 1)

            def shared_down(i):
                taken(pe, ("sh3", i // 4, KH - 1))
                ps = claim(("shout", i))
                for m in range(KH):
                    last = mm(ps[:, 0:D], hs[i // 4][:, m, i % 4 * P:(i % 4 + 1) * P], sw2[:, m, :], m == 0, m == KH - 1)
                last.then_inc(is_filled(("shout", i)), 1)

            pe.wait_ge(loaded["sw"], 64)
            for m in range(KH):
                shared_up("sh1", 0, m)
                shared_up("sh3", 0, m)
                if m == 0:
                    ps = claim(("rank",))
                    pe.wait_ge(oh_ready, 1)
                    mm(ps[:, 0:64], tri, route[:, 2, :], True, False)
                    mm(ps[:, 0:64], ones[:, :], route[:, 3, :], False, True).then_inc(is_filled(("rank",)), 1)
            for i in range(4):
                shared_down(i)
            pe.wait_ge(loaded["xd_rows"], 16)
            for g in range(4):
                ps = claim(("xdT", g))
                for k in range(KD):
                    for t in range(2):
                        last = nc.tensor.transpose(ps[:, k * D + t * P:k * D + (t + 1) * P],
                                                   xd[:, 2 * g + t, k * P:(k + 1) * P], ident)
                last.then_inc(is_filled(("xdT", g)), 1)

            def expert_up(e):
                pe.wait_ge(loaded["W1"], 16 * E)
                pe.wait_ge(loaded["W3"], 16 * E)
                taken(pe, ("xdT", e // 2))
                for name, w in (("e1", W1), ("e3", W3)):
                    ps = claim((name, e))
                    for m in range(KH):
                        for k in range(KD):
                            last = mm(ps[:, m * P:(m + 1) * P], w[:, e, k, m * P:(m + 1) * P],
                                      xdT[:, k, e, :], k == 0, k == KD - 1)
                    last.then_inc(is_filled((name, e)), 1)

            expert_up(0)
            for e in range(E):
                if e + 1 < E:
                    expert_up(e + 1)
                ps = claim(("eout", e))
                pe.wait_ge(loaded["W2"], 32 * E)
                taken(pe, ("e3", e))
                for m in range(KH):
                    last = mm(ps[:, 0:D], he[:, e % 2, m * P:(m + 1) * P], W2[:, e, m, :], m == 0, m == KH - 1)
                last.then_inc(is_filled(("eout", e)), 1)

            for n in range(8):
                pe.wait_ge(drained[n], plan.used[n])

            def scores(i, h):
                ps = claim(("S", i, h))
                g = h // REP
                pe.wait_ge(qk_split, rope_no[i, g] + 1)
                n = (i + 1) * P
                for at in range(0, n, 512):
                    end = min(at + 512, n)
                    for a, b in PAIRS:
                        mm(ps[:, at:end], qT[:, a, h, :], kT[:, b, g, at:end], (a, b) == PAIRS[0],
                           end < n and (a, b) == PAIRS[-1])
                mm(ps[:, i * P:n], ident_h[:, :], mask_h[:, :], False, True).then_inc(is_filled(("S", i, h)), 1)

            def project(job, chunk):
                i = job[1]
                pe.wait_ge(h3_split, i + 1)
                if i == 0:
                    pe.wait_ge(w_split, 2 * W_ORDER.index(chunk) + 2)
                ps = claim(job)
                for k in range(KD):
                    for a, b in PAIRS:
                        last = mm(ps, h3T[i % 2][:, a, k, :], wqkv[:, chunk, b, k, :], k == 0 and (a, b) == PAIRS[0],
                                  k == KD - 1 and (a, b) == PAIRS[-1])
                last.then_inc(is_filled(job), 1)

            def beside_pe(work):
                kind, i, *rest = work
                if kind in ("sh1", "sh3"):
                    shared_up(kind, i, *rest)
                elif kind == "shout":
                    shared_down(i)
                elif kind == "h3T":
                    pe.wait_ge(ln_done, ln_no["ln3", i] + 1)
                    ps = claim(work)
                    for k in range(KD):
                        last = nc.tensor.transpose(ps[:, k * P:(k + 1) * P], xn1[0][:, k * P:(k + 1) * P], ident)
                    last.then_inc(is_filled(work), 1)
                elif kind == "h4T":
                    pe.wait_ge(ln_done, ln_no["ln4", i] + 1)
                    ps = claim(work)
                    for k in range(KD):
                        last = nc.tensor.transpose(ps[:, k * P:(k + 1) * P], xn1[1][:, k * P:(k + 1) * P], ident)
                    last.then_inc(is_filled(work), 1)
                elif kind == "proj":
                    project(work, {"k": 8, "v": 9}.get(rest[0], rest[0]))
                elif kind == "gate":
                    project(work, 4 + rest[0])
                elif kind == "eT":
                    pe.wait_ge(tab_ready, i + 1)
                    ps = claim(work)
                    for a in range(2):
                        last = nc.tensor.transpose(ps[:, a * P:(a + 1) * P], rope_E[:, a, :], ident)
                    last.then_inc(is_filled(work), 1)
                elif kind == "qkT":
                    r_no = rope_no[i, rest[0]]
                    pe.wait_ge(rope_r, r_no + 1)
                    pe.wait_ge(rope_i, r_no + 1)
                    ps = claim(work)
                    for a in range(4):
                        last = nc.tensor.transpose(ps[:, a * P:(a + 1) * P], roped_of(r_no)[:, a, :], ident)
                    last.then_inc(is_filled(work), 1)
                elif kind == "oT":
                    g = rest[0]
                    taken(pe, ("O", i, 4 * g + 3))
                    ps = claim(work)
                    for a in range(4):
                        last = nc.tensor.transpose(ps[:, a * P:(a + 1) * P], osb[:, a * P:(a + 1) * P], ident)
                    last.then_inc(is_filled(work), 1)
                elif kind == "wo":
                    if i == 0:
                        pe.wait_ge(loaded["wo"], 16)
                    for g in range(4):
                        taken(pe, ("oT", i, g))
                    ps = claim(work)
                    for h in range(HQ):
                        last = mm(ps[:, 0:D], oT[:, h, :], wo[:, h, :], h == 0, h == HQ - 1)
                    last.then_inc(is_filled(work), 1)
                elif kind == "gu":
                    c = rest[0]
                    if i == 0 and c == 0:
                        pe.wait_ge(loaded["wffn"], 48)
                    taken(pe, ("h4T", i))
                    w = (wgate, wup)[c % 2]
                    ps = claim(work)
                    for k in range(KD):
                        last = mm(ps, h4T[:, k, :], w[:, k, c // 2 * 512:(c // 2 + 1) * 512], k == 0, k == KD - 1)
                    last.then_inc(is_filled(work), 1)
                elif kind == "hsT":
                    g = rest[0]
                    pe.wait_ge(sparse_ready, sparse_no(i))
                    ps = claim(work)
                    for a in range(4):
                        b = 4 * g + a
                        last = nc.tensor.transpose(ps[:, a * P:(a + 1) * P], sg[:, b * P:(b + 1) * P], ident)
                    last.then_inc(is_filled(work), 1)
                elif kind == "down":
                    for g in range(2):
                        taken(pe, ("hsT", i, g))
                    ps = claim(work)
                    for m in range(FF // P):
                        last = mm(ps[:, 0:D], hsT[:, m, :], wdown[:, m, :], m == 0, m == FF // P - 1)
                    last.then_inc(is_filled(work), 1)

            for att, beside in steps:
                if att == (0, 0):
                    for h in range(AHEAD):
                        scores(0, h)
                if att:
                    i, h = att
                    taken(pe, ("S", i, h))
                    for g, js in enumerate(groups(i)):
                        ps = claim(("PT", i, h, g))
                        for a, j in enumerate(js):
                            last = nc.tensor.transpose(ps[:, a * P:(a + 1) * P], pr[:, h % 2, j * P:(j + 1) * P], ident)
                        last.then_inc(is_filled(("PT", i, h, g)), 1)
                if att and after(att):
                    scores(*after(att))
                for work in beside:
                    beside_pe(work)
                if att:
                    ps = claim(("O", i, h))
                    if h == 0:
                        taken(pe, ("proj", i, "v"))
                    for g, js in enumerate(groups(i)):
                        taken(pe, ("PT", i, h, g))
                        for a, j in enumerate(js):
                            last = mm(ps[:, 0:DH], PT[:, pt_no[i, h, g] % 2, a * P:(a + 1) * P],
                                      v[:, j, h // REP * DH:(h // REP + 1) * DH], j == 0, j == i)
                    last.then_inc(is_filled(("O", i, h)), 1)
            assert next(order, None) is None

        @block.scalar
        def _(eng):
            marks = [0]

            def mark(ins):
                marks[0] += 1
                ins.then_inc(act, 1)

            def own():
                eng.wait_ge(act, marks[0])

            ac = nc.scalar.activation
            eng.wait_ge(loaded["vectors"], 16)
            ac(small[:, 0:4], c_cols, ACT.Silu).then_inc(sc_ready, 1)

            def h_modulated(which, g, shift, scale):
                job = ("hT", which, g)
                landed(eng, job)
                for k in range(KD):
                    last = ac(hT[:, g // 2, k, g % 2 * D:(g % 2 + 1) * D], bank(job)[:, k * D:(k + 1) * D], ACT.Identity,
                              bias=mod_col[:, shift + k:shift + k + 1], scale=mod_col[:, scale + k:scale + k + 1])
                last.then_inc(is_drained(job), 1)

            taken(eng, ("modcol", 0))
            for g in range(NT // 2):
                h_modulated("mix", g, 0, 2)

            def conv_act(n, m):
                if (n, m) == (0, 0):
                    eng.wait_ge(pool_init, 1)
                job = ("xbc", n, m)
                landed(eng, job)
                ac(xc[:, m, 3 + n * 512:3 + (n + 1) * 512], bank(job), ACT.Copy).then_inc(conv_in, 1)
                ac(xT[:, m, n * 512:(n + 1) * 512], bank(job), ACT.Copy, scale=conv_w[:, m, 3:4]).then_inc(is_drained(job), 1)

            def conv_silu_act(n, m):
                cols = slice(n * 512, (n + 1) * 512)
                eng.wait_ge(conv_done, 5 * n + m + 1)
                if m < 4:
                    ac(xT[:, m, cols], xT[:, m, cols], ACT.Silu, bias=conv_b[:, m:m + 1]).then_inc(conv_silu, 1)
                else:
                    ac(BT[0:NS, cols], xT[0:NS, m, cols], ACT.Silu, bias=conv_b[0:NS, m:m + 1])
                    ac(CT[0:NS, cols], xT[NS:P, m, cols], ACT.Silu, bias=conv_b[NS:P, m:m + 1]).then_inc(conv_silu, 1)

            for n in range(2):
                for m in range(5):
                    conv_act(n, m)
                    if m:
                        conv_silu_act(n, m - 1)
                for i in range(4 * n, 4 * n + 4):
                    landed(eng, ("z", i))
                    ac(zs[:, i, :], bank(("z", i)), ACT.Silu).then_inc(is_drained(("z", i)), 1)
                    if i == 4 * n:
                        conv_silu_act(n, 4)

            ac(small[:, 4:8], a_log, ACT.Exp).then_inc(a_exp, 1)
            eng.wait_ge(dt_abs, 1)
            ac(dtb[:, 2, :], dtb[:, 1, :], ACT.Exp, scale=-1.0).then_inc(dt_exp, 1)

            def front(c):
                if c >= 2:
                    eng.wait_ge(xdt_ready, 2 * c - 2)
                landed(eng, ("xtok", c))
                ac(x_sb[:, c % 2], bank(("xtok", c)).rearrange("p (h d) -> p h d", h=NH), ACT.Copy).then_inc(is_drained(("xtok", c)), 1)
                if c >= 2:
                    taken(eng, ("state", c - 2))
                landed(eng, ("misc", c))
                ac(es[:, c % 2, :], bank(("misc", c))[:, 256:264], ACT.Exp)
                ac(B_tok[:, c % 2, :], bank(("misc", c))[:, 0:NS], ACT.Copy).then_inc(misc_act, 1)
                if c:
                    eng.wait_ge(xs_ready, c)
                landed(eng, ("seg", c))
                ac(Lm, bank(("seg", c)).rearrange("p (h d) -> p h d", h=NH), ACT.Exp).then_inc(is_drained(("seg", c)), 1)

            front(0)
            for c in range(NT):
                if c + 1 < NT:
                    front(c + 1)
                eng.wait_ge(yg_ready, c + 1)
                ac(sq_out, yg[:, c % 2].rearrange("p h d -> p (h d)"), ACT.Square, accum_out=small[:, 8 + c:9 + c]).then_inc(yg_sq, 1)
                for g, at in MOE_HT_AT.items():
                    if at == c:
                        h_modulated("moe", g, 4, 6)
            eng.wait_ge(x_mixed, NT)
            ac(small[:, 40:41], small[:, 8:9], ACT.Copy).then_inc(moe_free, 1)

            for g in range(NT // 2):
                if g not in MOE_HT_AT:
                    h_modulated("moe", g, 4, 6)
            eng.wait_ge(route_d, 1)
            ac(route[:, 4, :], route[:, 1, :], ACT.Exp).then_inc(route_e, 1)

            def shared_act(n, m):
                if m >= 2:
                    taken(eng, ("sh3", n, m - 2))
                elif n:
                    taken(eng, ("e3", E - 1))
                landed(eng, ("sh1", n, m))
                ac(s1_of(n, m), bank(("sh1", n, m)), ACT.Silu).then_inc(is_drained(("sh1", n, m)), 1)

            for m in range(KH):
                shared_act(0, m)
            def w_hi_half(n):
                eng.wait_ge(w_full[n % 4], 16 * (n // 4 + 1))
                ac(wqkv[:, W_ORDER[n // 2], 0, n % 2, :], staged[n % 4], ACT.Copy, scale=W_SCALE).then_inc(w_hi, 1)

            for n in range(4):
                w_hi_half(n)
            for g in range(4):
                job = ("xdT", g)
                landed(eng, job)
                for k in range(KD):
                    last = ac(xdT[:, k, 2 * g:2 * g + 2, :], bank(job)[:, k * D:(k + 1) * D].rearrange("p (e s) -> p e s", e=2),
                              ACT.Identity, bias=mod_col[:, 4 + k:5 + k], scale=mod_col[:, 6 + k:7 + k])
                last.then_inc(is_drained(job), 1)

            def expert_act(e):
                if e >= 2:
                    taken(eng, ("e3", e - 2))
                landed(eng, ("e1", e))
                ac(se[:, e % 2, :], bank(("e1", e))[:, 0:HP], ACT.Silu).then_inc(is_drained(("e1", e)), 1)

            expert_act(0)
            for e in range(E):
                if e + 1 < E:
                    expert_act(e + 1)
                landed(eng, ("eout", e))
                ac(oe[:, e, :], bank(("eout", e))[:, 0:D], ACT.Copy).then_inc(is_drained(("eout", e)), 1)
                taken(eng, ("eout", e))
                eng.dma_start(oe_d[e * CAP:(e + 1) * CAP, :], oe[:, e, :]).then_inc(oe_stored, 16)
                for n in range(4 + 2 * e, 6 + 2 * e):
                    w_hi_half(n)

            def softmax(i, h):
                no = i * HQ + h
                n = (i + 1) * P
                b = no % 4
                eng.wait_ge(maxed, no + 1)
                ac(nmax_scaled[:, b:b + 1], nmax[:, b:b + 1], ACT.Copy, scale=S_UNSCALE).then_inc(max_scaled, 1)
                eng.wait_ge(max_scaled, no + 1)
                landed(eng, ("S", i, h))
                if no >= 2:
                    pi, ph = divmod(no - 2, HQ)
                    landed(eng, ("PT", pi, ph, len(groups(pi)) - 1))
                if no >= 4:
                    taken(eng, ("O", *divmod(no - 4, HQ)))
                ac(pr[:, h % 2, 0:n], bank(("S", i, h))[:, 0:n], ACT.Exp, bias=nmax_scaled[:, b:b + 1],
                   scale=S_UNSCALE, accum_out=rsum[:, no % 4:no % 4 + 1]).then_inc(is_drained(("S", i, h)), 1)

            def beside_act(work):
                kind, i, *rest = work
                ps = bank(work) if work in plan.turn else None
                if kind == "sh1":
                    shared_act(i, *rest)
                elif kind == "h3T":
                    if i >= 2:
                        landed(eng, ("gate", i - 2, 3))
                    if i:
                        eng.wait_ge(h3_split, i)
                    landed(eng, work)
                    for out in (h3T[i % 2][:, 0], h3_full):
                        for k in range(KD):
                            last = ac(out[:, k, :], ps[:, k * P:(k + 1) * P], ACT.Identity,
                                      bias=mod_col[:, 8 + k:9 + k], scale=mod_col[:, 10 + k:11 + k])
                    last.then_inc(is_drained(work), 1)
                elif kind == "h4T":
                    if i:
                        landed(eng, ("gu", i - 1, 3))
                    landed(eng, work)
                    for k in range(KD):
                        last = ac(h4T[:, k, :], ps[:, k * P:(k + 1) * P], ACT.Identity,
                                  bias=mod_col[:, 12 + k:13 + k], scale=mod_col[:, 14 + k:15 + k])
                    last.then_inc(is_drained(work), 1)
                elif kind == "proj" and rest[0] == "v":
                    landed(eng, work)
                    ac(v[:, i, :], ps, ACT.Copy, scale=1 / W_SCALE).then_inc(is_drained(work), 1)
                elif kind == "proj":
                    r_no = rope_no[i, rest[0]]
                    if r_no > 4:
                        eng.wait_ge(rope_r, r_no)
                        eng.wait_ge(rope_i, r_no)
                    landed(eng, work)
                    ac(raw_of(r_no), ps.rearrange("p (h d) -> p h d", h=4), ACT.Copy,
                       scale=1 / W_SCALE).then_inc(is_drained(work), 1)
                elif kind == "split":
                    r_no, half = rope_no[i, rest[0]], qk_of(work)
                    taken(eng, ("qkT", i, rest[0]))
                    ac(half(0), sum_of(r_no), ACT.Copy).then_inc(qk_hi, 1)
                elif kind == "gate":
                    no = 4 * i + rest[0]
                    if no >= 2:
                        pi, pg = divmod(no - 2, 4)
                        taken(eng, ("O", pi, 4 * pg + 3))
                    landed(eng, work)
                    ac(gate[:, no % 2, :], ps, ACT.Tanh, scale=0.5 / W_SCALE).then_inc(is_drained(work), 1)
                elif kind == "eT":
                    if i:
                        taken(eng, ("qkT", i - 1, 3))
                    landed(eng, work)
                    ac(eT, ps[:, 0:D].rearrange("p (a t) -> p a t", a=2), ACT.Copy).then_inc(is_drained(work), 1)
                elif kind == "oT":
                    g = rest[0]
                    if i:
                        landed(eng, ("wo", i - 1))
                    landed(eng, work)
                    ac(oT[:, 4 * g:4 * g + 4, :], ps.rearrange("p (h t) -> p h t", h=4), ACT.Copy).then_inc(is_drained(work), 1)
                elif kind == "gu" and rest[0] % 2 == 0:
                    half = rest[0] // 2
                    if i:
                        eng.wait_ge(sparse_ready, sparse_no(i - 1))
                    landed(eng, work)
                    ac(tb[:, half * 512:(half + 1) * 512], ps, ACT.Tanh, scale=0.5).then_inc(gu_tanh, 1)
                elif kind == "hsT":
                    g = rest[0]
                    if i:
                        landed(eng, ("down", i - 1))
                    landed(eng, work)
                    ac(hsT[:, 4 * g:4 * g + 4, :], ps.rearrange("p (h t) -> p h t", h=4), ACT.Copy).then_inc(is_drained(work), 1)

            for att, beside in steps:
                if att == (0, 0):
                    for h in range(AHEAD):
                        softmax(0, h)
                if att:
                    i, h = att
                    no = pt_no[i, h, 0]
                    if no >= 2:
                        landed(eng, ("O", *pt_key[no - 2][:2]))
                    n = len(groups(i)[0]) * P
                    landed(eng, ("PT", i, h, 0))
                    ac(PT[:, no % 2, 0:n], bank(("PT", i, h, 0))[:, 0:n], ACT.Copy).then_inc(is_drained(("PT", i, h, 0)), 1)
                if att and after(att):
                    softmax(*after(att))
                for work in beside:
                    beside_act(work)

        @block.vector
        def _(eng):
            marks = [0]

            def mark(ins):
                marks[0] += 1
                ins.then_inc(dve, 1)

            def own():
                eng.wait_ge(dve, marks[0])

            ts, tt, stt = nc.vector.tensor_scalar, nc.vector.tensor_tensor, nc.vector.scalar_tensor_tensor

            nc.vector.memset(ones[:, :], 1.0)
            nc.vector.memset(half_neg[:, :], -0.5)
            nc.vector.memset(zeros, 0.0).then_inc(dve_init, 1)
            eng.wait_ge(dve_init, 1)
            eng.wait_ge(loaded["consts"], 16)
            mark(nc.vector.tensor_copy(ident_h[:, :], ident))
            mark(tt(xtmp[:, 0:P], tri, ident, ALU.subtract))
            own()
            mark(ts(mask_h[:, :], xtmp[:, 0:P], MASKED, None, ALU.mult))
            eng.wait_ge(sc_ready, 1)
            for s in range(4):
                last = ts(sc_b[:, s, :], ones[:, :], small[:, s:s + 1], None, ALU.mult)
            last.then_inc(scb_ready, 1)

            def stats(key, i):
                if key == "moe":
                    eng.wait_ge(x_mixed, i + 1)
                s = ln_no[key, i] % 4
                if ln_no[key, i] >= 4:
                    eng.wait_ge(ln_done, ln_no[key, i] - 3)
                mark(nc.vector.bn_stats(ln_st[:, s, :], x[:, i, :]))
                own()
                nc.vector.bn_aggr(ln_mv[:, s, :], ln_st[:, s, :]).then_inc(ln_stats, 1)

            def normalise(key, i, out):
                n = ln_no[key, i]
                eng.wait_ge(ln_scaled, n + 1)
                eng.wait_ge(ln_stats, n + 1)
                ts(out, x[:, i, :], ln_mv[:, n % 4, 0:1], ln_rstd[:, n % 4:n % 4 + 1],
                   ALU.subtract, ALU.mult).then_inc(ln_done, 1)

            eng.wait_ge(loaded["x"], 16)
            for i in range(NT + 2):
                if i < NT:
                    stats("mix", i)
                if i >= 2:
                    normalise("mix", i - 2, xn[:, i - 2, :])

            def mod_columns(l):
                job = ("modcol", l)
                landed(eng, job)
                cols = mod_col[:, 8 * l:8 * l + 8]
                mark(nc.vector.tensor_copy(cols, bank(job)[:, 0:8]))
                own()
                scale = cols.rearrange("p (s v k) -> p s v k", s=2, v=2)[:, :, 1, :]
                ts(scale, scale, 1.0, None, ALU.add).then_inc(is_drained(job), 1)

            mod_columns(0)

            job = ("dt",)
            landed(eng, job)
            bc8 = lambda t: t.unsqueeze(1).to_broadcast([P, NT, NH])
            d3 = lambda n: dtb[:, n, :].rearrange("p (i h) -> p i h", h=NH)
            tt(d3(0), bank(job)[:, 0:32].rearrange("p (i h) -> p i h", h=NH), bc8(dt_bias),
               ALU.add).then_inc(is_drained(job), 1)
            taken(eng, job)
            stt(dtb[:, 1, :], dtb[:, 0, :], -1.0, dtb[:, 0, :], ALU.mult, ALU.max).then_inc(dt_abs, 1)

            def conv(n, m):
                eng.wait_ge(conv_in, 5 * n + m + 1)
                taken(eng, ("xbc", n, m))
                acc = xT[:, m, n * 512:(n + 1) * 512]
                for j in range(3):
                    ins = stt(acc, xc[:, m, n * 512 + j:n * 512 + j + 512], conv_w[:, m, j:j + 1], acc, ALU.mult, ALU.add)
                    if j < 2:
                        mark(ins)
                        own()
                ins.then_inc(conv_done, 1)

            for n in range(2):
                for m in range(5):
                    conv(n, m)

            eng.wait_ge(dt_exp, 1)
            ts(dt_as_relu, dtb[:, 0, :], 0.0, None, ALU.max)
            mark(ts(dtb[:, 3, :], dtb[:, 2, :], 2.0, None, ALU.add))
            own()
            mark(nc.vector.reciprocal(dtb[:, 4, :], dtb[:, 3, :]))
            own()
            mark(tt(dtb[:, 5, :], dtb[:, 4, :], dtb[:, 2, :], ALU.mult))
            own()
            mark(tt(dtb[:, 6, :], dtb[:, 5, :], dtb[:, 5, :], ALU.mult))
            own()
            mark(ts(dtb[:, 7, :], dtb[:, 6, :], 1.0 / 17, None, ALU.mult))
            for d in (15, 13, 11, 9, 7, 5, 3):
                own()
                mark(stt(dtb[:, 7, :], dtb[:, 7, :], 1.0 / d, dtb[:, 6, :], ALU.add, ALU.mult))
            own()
            mark(stt(dtb[:, 7, :], dtb[:, 7, :], 1.0, dtb[:, 5, :], ALU.add, ALU.mult))
            own()
            mark(stt(dtb[:, 9, :], dtb[:, 7, :], 2.0, dt_as_relu, ALU.mult, ALU.add))
            own()
            eng.wait_ge(a_exp, 1)
            stt(d3(10), d3(9), -1.0, bc8(small[:, 4:8]), ALU.mult, ALU.mult).then_inc(dt_ready, 1)

            def over_heads(t):
                return t.unsqueeze(1).to_broadcast([P, NH, P])

            def front(c):
                b = c % 2
                job = ("misc", c)
                landed(eng, job)
                eng.wait_ge(misc_act, c + 1)
                if c:
                    eng.wait_ge(mt_ready, c)
                tt(Gm, bank(job)[:, P:2 * P], tri, ALU.mult).then_inc(is_drained(job), 1)
                taken(eng, job)
                taken(eng, ("seg", c))
                tt(MT[:, b], Lm, over_heads(Gm), ALU.mult).then_inc(mt_ready, 1)
                eng.wait_ge(xdt_ready, 2 * c + 2)
                tt(Xs[:, b], Xdt[:, b], Lm[:, :, P - 1].unsqueeze(2).to_broadcast([P, NH, P]), ALU.mult).then_inc(xs_ready, 1)

            def turn_yg(c):
                job = ("ygT", c)
                landed(eng, job)
                if c == 0:
                    eng.wait_ge(zeroed, 16)
                tt(ygT, bank(job).rearrange("p (k t) -> p k t", k=4), norm_w.unsqueeze(2).to_broadcast([P, 4, P]),
                   ALU.mult).then_inc(is_drained(job), 1)

            def mix_out(c):
                job = ("mixout", c)
                landed(eng, job)
                eng.wait_ge(yg_rstd, c + 1)
                stt(xtmp[:, :], bank(job)[:, 0:D], small[:, 24 + c:25 + c], g_row[:, 0, 0:D], ALU.mult, ALU.mult).then_inc(is_drained(job), 1)
                taken(eng, job)
                tt(x[:, c, :], x[:, c, :], xtmp[:, :], ALU.add).then_inc(x_mixed, 1)

            mod_columns(1)
            for l in range(2):
                job = ("modrow", l)
                landed(eng, job)
                nc.vector.tensor_copy(g_row[:, l, :], bank(job)).then_inc(is_drained(job), 1)
                taken(eng, job)
                mark(stt(g_abs, g_row[:, l, :], -1.0, g_row[:, l, :], ALU.mult, ALU.max))
                own()
                mark(ts(g_abs, g_abs, 0.25, None, ALU.max))
                mark(ts(g_row[:, l, :], g_row[:, l, :], 0.0, 2.0, ALU.is_ge, ALU.mult))
                own()
                stt(g_row[:, l, :], g_row[:, l, :], -1.0, g_abs, ALU.add, ALU.mult).then_inc(g_ready, 1)
                eng.wait_ge(g_ready, l + 1)
            front(0)
            for c in range(NT):
                b = c % 2
                if c:
                    eng.wait_ge(yg_ready, c)
                job = ("ydiag", c)
                landed(eng, job)
                tt(y1, bank(job).rearrange("p (h d) -> p h d", h=NH), xD[:, b], ALU.add).then_inc(is_drained(job), 1)
                taken(eng, job)
                job = ("yoff", c)
                landed(eng, job)
                for h in range(NH):
                    last = stt(y1[:, h, :], bank(job)[:, h * P:(h + 1) * P], es[:, b, h:h + 1], y1[:, h, :], ALU.mult, ALU.add)
                last.then_inc(is_drained(job), 1)
                job = ("state", c)
                landed(eng, job)
                if c:
                    taken(eng, ("state", c - 1))
                for h in range(NH):
                    last = stt(S[0:NS, 1 - b, h, :], S[0:NS, b, h, :], es[0:NS, b, 4 + h:5 + h],
                               bank(job)[0:NS, h * P:(h + 1) * P], ALU.mult, ALU.add)
                last.then_inc(is_drained(job), 1)
                if c:
                    turn_yg(c - 1)
                if c + 1 < NT:
                    front(c + 1)
                if c:
                    mix_out(c - 1)
                    stats("moe", c - 1)
                if c >= 3:
                    normalise("moe", c - 3, xn[:, c - 3, :])
            turn_yg(NT - 1)
            mix_out(NT - 1)
            stats("moe", NT - 1)
            for i in range(NT - 3, NT):
                normalise("moe", i, xn[:, i, :])
            eng.wait_ge(moe_free, 2)

            r3 = lambda n: route[:, n, :].rearrange("p (i e) -> p i e", e=E)
            over_e = lambda n: rt8[:, n, :].unsqueeze(2).to_broadcast([P, NT, E])
            job = ("logits",)
            landed(eng, job)
            lg = bank(job)[:, 0:64].rearrange("p (i e) -> p i e", e=E)
            mark(nc.vector.reduce_max(rt8[:, 0, :], lg, AX_X))
            own()
            mark(tt(r3(0), lg, over_e(0), ALU.is_equal))
            tt(r3(1), lg, over_e(0), ALU.subtract).then_inc(is_drained(job), 1)
            taken(eng, job)
            nc.vector.tensor_copy(rt8[:, 8, :], rt8[:, 0, :]).then_inc(route_d, 1)
            own()
            mark(tt(route[:, 0, :], route[:, 0, :], rank_weight, ALU.mult))
            own()
            mark(nc.vector.reduce_max(rt8[:, 1, :], r3(0), AX_X))
            own()
            mark(tt(r3(2), r3(0), over_e(1), ALU.is_equal))
            mark(nc.vector.memset(route[:, 3, 0:E], 0.0))
            own()
            for i in range(1, NT):
                ins = tt(route[:, 3, i * E:(i + 1) * E], route[:, 3, (i - 1) * E:i * E],
                         route[:, 2, (i - 1) * E:i * E], ALU.add)
                if i < NT - 1:
                    mark(ins)
                    own()
            ins.then_inc(oh_ready, 1)
            job = ("rank",)
            landed(eng, job)
            eng.wait_ge(oh_ready, 1)
            tt(route[:, 0, :], bank(job)[:, 0:64], route[:, 2, :], ALU.mult).then_inc(is_drained(job), 1)
            taken(eng, job)
            mark(nc.vector.reduce_sum(rt8[:, 2, :], r3(0), AX_X))
            mark(tt(route[:, 3, :], route[:, 2, :], expert_base, ALU.mult))
            own()
            mark(nc.vector.reduce_sum(rt8[:, 3, :], r3(3), AX_X))
            mark(ts(rt8[:, 4, :], rt8[:, 2, :], CAP + 0.5, None, ALU.is_le))
            eng.wait_ge(route_e, 1)
            mark(nc.vector.reduce_sum(rt8[:, 5, :], r3(4), AX_X))
            own()
            mark(stt(rt8[:, 3, :], rt8[:, 2, :], -1.0, rt8[:, 3, :], ALU.add, ALU.add))
            mark(ts(rt8[:, 6, :], rt8[:, 4, :], -NEVER, NEVER, ALU.mult, ALU.add))
            mark(nc.vector.reciprocal(rt8[:, 5, :], rt8[:, 5, :]))
            own()
            mark(tt(rt8[:, 6, :], rt8[:, 6, :], rt8[:, 3, :], ALU.add))
            mark(tt(rt8[:, 7, :], rt8[:, 5, :], rt8[:, 4, :], ALU.mult))
            own()
            mark(nc.vector.tensor_copy(slot_u[:, 0, :], rt8[:, 6, :]))
            ts(slot_u[:, 1, :], rt8[:, 6, :], float(E * CAP - 1), None, ALU.min).then_inc(route_done, 1)

            def shared_units(n, m):
                job = ("sh3", n, m)
                landed(eng, job)
                taken(eng, ("sh1", n, m))
                tt(hs[n][:, m, :], bank(job), s1_of(n, m), ALU.mult).then_inc(is_drained(job), 1)

            added = {"shared": 0, "moe": 0}

            def xtmp_free():
                for counter, n in ((x_shared, added["shared"]), (x_moe, added["moe"])):
                    if n:
                        eng.wait_ge(counter, n)

            def shared_add(i):
                job = ("shout", i)
                landed(eng, job)
                xtmp_free()
                tt(xtmp[:, :], bank(job)[:, 0:D], g_row[:, 0, D:2 * D], ALU.mult).then_inc(is_drained(job), 1)
                taken(eng, job)
                tt(x[:, i, :], x[:, i, :], xtmp[:, :], ALU.add).then_inc(x_shared, 1)
                added["shared"] += 1

            def combine(i):
                eng.wait_ge(gathered[i], 16)
                xtmp_free()
                assert added["shared"] > i
                mark(stt(xtmp[:, :], og[:, i, :], rt8[:, 7, i:i + 1], g_row[:, 0, D:2 * D], ALU.mult, ALU.mult))
                own()
                tt(x[:, i, :], x[:, i, :], xtmp[:, :], ALU.add).then_inc(x_moe, 1)
                added["moe"] += 1

            for m in range(KH):
                shared_units(0, m)
            for i in range(4):
                shared_add(i)

            def w_lo_half(n):
                eng.wait_ge(w_hi, n + 1)
                hi, lo = (wqkv[:, W_ORDER[n // 2], v, n % 2, :] for v in range(2))
                stt(lo, staged[n % 4], W_SCALE, hi, ALU.mult, ALU.subtract).then_inc(w_split, 1)

            for n in range(4):
                w_lo_half(n)
            for e in range(E):
                if e >= 2:
                    landed(eng, ("eout", e - 2))
                job = ("e3", e)
                landed(eng, job)
                taken(eng, ("e1", e))
                tt(he[:, e % 2, :], bank(job)[:, 0:HP], se[:, e % 2, :], ALU.mult).then_inc(is_drained(job), 1)
                if e:
                    for n in range(2 + 2 * e, 4 + 2 * e):
                        w_lo_half(n)
            for n in range(W_PARTS - 2, W_PARTS):
                w_lo_half(n)

            def row_max(i, h):
                no = i * HQ + h
                landed(eng, ("S", i, h))
                if no >= 4:
                    taken(eng, ("S", *divmod(no - 4, HQ)))
                nc.vector.reduce_max(nmax[:, no % 4:no % 4 + 1], bank(("S", i, h))[:, 0:(i + 1) * P], AX_X,
                                     negate=True).then_inc(maxed, 1)

            def beside_dve(work):
                kind, i, *rest = work
                ps = bank(work) if work in plan.turn else None
                if kind == "sh3":
                    shared_units(i, *rest)
                elif kind == "shout":
                    shared_add(i)
                elif kind == "combine":
                    combine(i)
                elif kind in ("ln3", "ln4"):
                    eng.wait_ge(*((x_att, i + 1) if kind == "ln4" else (x_moe, i + 1)))
                    stats(kind, i)
                    if i:
                        landed(eng, ({"ln3": "h3T", "ln4": "h4T"}[kind], i - 1))
                    normalise(kind, i, xn1[0 if kind == "ln3" else 1])
                elif kind == "proj" and rest[0] != "v":
                    r_no = rope_no[i, rest[0]]
                    taken(eng, work)
                    for a in range(4):
                        last = nc.vector.bn_stats(q_st[:, r_no % 2, a, :], raw_of(r_no)[:, a, :])
                    mark(last)
                    own()
                    for a in range(4):
                        last = nc.vector.bn_aggr(q_mv[:, r_no % 2, a, :], q_st[:, r_no % 2, a, :])
                    last.then_inc(q_stats, 1)
                elif kind == "rope":
                    r_no = rope_no[i, rest[0]]
                    b, qk = r_no % 2, int(rest[0] == "k")
                    eng.wait_ge(q_rstd, r_no + 1)
                    eng.wait_ge(q_stats, r_no + 1)
                    for a in range(4):
                        last = ts(raw_of(r_no)[:, a, :], raw_of(r_no)[:, a, :], q_mv[:, b, a, 0:1], q_rs[:, b, a:a + 1],
                                  ALU.subtract, ALU.mult)
                    last.then_inc(q_norm, 1)
                    eng.wait_ge(q_norm, r_no + 1)
                    eng.wait_ge(tab_ready, i + 1)
                    if r_no:
                        eng.wait_ge(rope_r, r_no)
                    table = lambda s: rt[:, s, qk, :].unsqueeze(1).to_broadcast([P, 4, 64])
                    mark(tt(t_r[:, 0], raw_of(r_no)[:, :, 0:64], table(0), ALU.mult))
                    mark(tt(t_r[:, 1], raw_of(r_no)[:, :, 64:128], table(1), ALU.mult))
                    own()
                    if r_no > 4:
                        eng.wait_ge(qk_split, r_no)
                    tt(roped_of(r_no)[:, :, 0:64], t_r[:, 0], t_r[:, 1], ALU.subtract).then_inc(rope_r, 1)
                elif kind == "qkT":
                    c = rest[0]
                    r_no = rope_no[i, c]
                    taken(eng, ("eT", i))
                    landed(eng, work)
                    src = ps.rearrange("p (h t) -> p h t", h=4)
                    e = eT[:, int(c == "k"), :].unsqueeze(1).to_broadcast([P, 4, P])
                    tt(sum_of(r_no), src, e, ALU.add).then_inc(is_drained(work), 1)
                elif kind == "wo":
                    landed(eng, work)
                    eng.wait_ge(*((x_out, i) if i else (x_moe, NT)))
                    tt(xtmp[:, :], ps[:, 0:D], g_row[:, 1, 0:D], ALU.mult).then_inc(is_drained(work), 1)
                    taken(eng, work)
                    tt(x[:, i, :], x[:, i, :], xtmp[:, :], ALU.add).then_inc(x_att, 1)
                elif kind == "gu":
                    c = rest[0]
                    cols = slice(c // 2 * 512, (c // 2 + 1) * 512)
                    landed(eng, work)
                    if c % 2 == 0:
                        eng.wait_ge(gu_tanh, 2 * i + c // 2 + 1)
                        if i:
                            landed(eng, ("hsT", i - 1, 1))
                        stt(sg[:, cols], tb[:, cols], 1.0, ps, ALU.add, ALU.mult).then_inc(is_drained(work), 1)
                    else:
                        taken(eng, ("gu", i, c - 1))
                        tt(sg[:, cols], sg[:, cols], ps, ALU.mult).then_inc(is_drained(work), 1)
                elif kind == "sparse":
                    a4 = tb[:, :].rearrange("p (g a b) -> p g a b", a=2, b=2)
                    c01, c23, c02, c13, c03, c12 = (cmp_h[:, n, :] for n in range(6))
                    sp_ = [spt_h[:, n, :] for n in range(4)]
                    if rest[0] == 0:
                        taken(eng, ("gu", i, 3))
                        mark(stt(tb[:, :], sg[:, :], -1.0, sg[:, :], ALU.mult, ALU.max))
                    elif rest[0] == 1:
                        own()
                        c01_23, c02_13 = cmp_h[:, 0:2, :], cmp_h[:, 2:4, :]
                        mark(tt(c01_23.rearrange("p c g -> p g c"), a4[:, :, :, 0], a4[:, :, :, 1], ALU.is_ge))
                        mark(tt(c02_13.rearrange("p c g -> p g c"), a4[:, :, 0, :], a4[:, :, 1, :], ALU.is_ge))
                        mark(tt(c03, a4[:, :, 0, 0], a4[:, :, 1, 1], ALU.is_ge))
                        mark(tt(c12, a4[:, :, 0, 1], a4[:, :, 1, 0], ALU.is_ge))
                    elif rest[0] == 2:
                        if i:
                            landed(eng, ("down", i - 1))
                        own()
                        mark(tt(sp_[0], c01, c02, ALU.add))
                        mark(tt(sp_[1], c12, c13, ALU.add))
                        mark(tt(sp_[2], c02, c12, ALU.add))
                        mark(tt(sp_[3], c03, c13, ALU.add))
                        own()
                        mark(tt(sp_[0], sp_[0], c03, ALU.add))
                        mark(tt(sp_[1], sp_[1], c01, ALU.subtract))
                        mark(tt(sp_[2], sp_[2], c23, ALU.subtract))
                        mark(tt(sp_[3], sp_[3], c23, ALU.add))
                    else:
                        own()
                        h4 = sg[:, :].rearrange("p (g j) -> p g j", j=4)
                        for j, (op, at) in enumerate(((ALU.is_ge, 1.5), (ALU.is_ge, 0.5), (ALU.is_lt, 0.5), (ALU.is_lt, 1.5))):
                            last = stt(h4[:, :, j], sp_[j], at, h4[:, :, j], op, ALU.mult)
                        last.then_inc(sparse_ready, 1)
                elif kind == "down":
                    landed(eng, work)
                    eng.wait_ge(x_att, i + 1)
                    stt(xtmp[:, :], ps[:, 0:D], 0.5, g_row[:, 1, D:2 * D], ALU.mult, ALU.mult).then_inc(is_drained(work), 1)
                    taken(eng, work)
                    tt(x[:, i, :], x[:, i, :], xtmp[:, :], ALU.add).then_inc(x_out, 1)

            for att, beside in steps:
                if att == (0, 0):
                    for h in range(AHEAD):
                        row_max(0, h)
                if att:
                    i, h = att
                    no = i * HQ + h
                    g = h // 4
                    if i >= 4:
                        n_pt = pt_no[i, h, 1]
                        landed(eng, ("O", *pt_key[n_pt - 2][:2]))
                        n = len(groups(i)[1]) * P
                        landed(eng, ("PT", i, h, 1))
                        nc.vector.tensor_copy(PT[:, n_pt % 2, 0:n], bank(("PT", i, h, 1))[:, 0:n]).then_inc(is_drained(("PT", i, h, 1)), 1)
                if att and after(att):
                    row_max(*after(att))
                for work in beside:
                    beside_dve(work)
                if att:
                    taken(eng, ("S", i, h))
                    mark(nc.vector.reciprocal(rinv[:, no % 4:no % 4 + 1], rsum[:, no % 4:no % 4 + 1]))
                    own()
                    eng.wait_ge(gate_ready, 4 * i + g + 1)
                    if h % 4 == 0 and 4 * i + g:
                        landed(eng, ("oT", *divmod(4 * i + g - 1, 4)))
                    landed(eng, ("O", i, h))
                    col = slice(h % 4 * P, (h % 4 + 1) * P)
                    stt(osb[:, col], bank(("O", i, h))[:, 0:DH], rinv[:, no % 4:no % 4 + 1],
                        gate[:, g % 2, col], ALU.mult, ALU.mult).then_inc(is_drained(("O", i, h)), 1)

        @block.gpsimd
        def _(eng):
            marks = [0]

            def mark(ins):
                marks[0] += 1
                ins.then_inc(pool, 1)

            def own():
                eng.wait_ge(pool, marks[0])

            ts, tt = nc.gpsimd.tensor_scalar, nc.gpsimd.tensor_tensor
            nc.gpsimd.memset(sw1[:, :, H:HP], 0.0)
            nc.gpsimd.memset(S[0:NS, 0], 0.0)
            mark(nc.gpsimd.memset(sw3[:, :, H:HP], 0.0))
            own()
            mark(nc.gpsimd.memset(sw2[H - 2 * P:P, 2, :], 0.0))
            own()
            nc.gpsimd.memset(xc[:, :, 0:3], 0.0).then_inc(pool_init, 1)

            def inv_sqrt(out, in_, tmp, mul, eps, n):
                mark(ts(tmp, in_, mul, eps, ALU.mult, ALU.add))
                own()
                return tt(out, tmp, half_neg[:, 0:n], ALU.pow)

            def scale_ln(n):
                s = n % 4
                eng.wait_ge(ln_stats, n + 1)
                inv_sqrt(ln_rstd[:, s:s + 1], ln_mv[:, s, 1:2], ln_t[:, s:s + 1], 1.0, 1e-5, 1).then_inc(ln_scaled, 1)

            eng.wait_ge(dve_init, 1)
            for i in range(NT):
                scale_ln(i)

            def over_p(t):
                return t.unsqueeze(2).to_broadcast([P, NH, P])

            def front(c):
                b = c % 2
                if c >= 2:
                    landed(eng, ("seg", c - 2))
                tt(M1[:, b], stril.unsqueeze(1).to_broadcast([P, NH, P]), over_p(a_dt(c)), ALU.mult).then_inc(m1_ready, 1)
                taken(eng, ("xtok", c))
                if c >= 2:
                    taken(eng, ("ydiag", c - 2))
                    eng.wait_ge(xs_ready, c - 1)
                tt(xD[:, b], x_sb[:, b], over_p(d_skip), ALU.mult).then_inc(xdt_ready, 1)
                tt(Xdt[:, b], x_sb[:, b], over_p(dtb[:, 9, c * NH:(c + 1) * NH]), ALU.mult).then_inc(xdt_ready, 1)

            eng.wait_ge(dt_ready, 1)
            front(0)
            for c in range(NT):
                if c + 1 < NT:
                    front(c + 1)
                if c == 1:
                    eng.wait_ge(g_ready, 2)
                    nc.gpsimd.memset(W1[:, :, :, H:HP], 0.0)
                    nc.gpsimd.memset(W3[:, :, :, H:HP], 0.0).then_inc(pads, 1)
                if c >= 2:
                    landed(eng, ("ygT", c - 2))
                taken(eng, ("yoff", c))
                taken(eng, ("z", c))
                tt(yg[:, c % 2], y1, zs[:, c, :].rearrange("p (h d) -> p h d", h=NH), ALU.mult).then_inc(yg_ready, 1)
                eng.wait_ge(yg_sq, c + 1)
                inv_sqrt(small[:, 24 + c:25 + c], small[:, 8 + c:9 + c], small[:, 32:33], 1.0 / DI, 1e-5, 1).then_inc(yg_rstd, 1)
                if c >= 2:
                    scale_ln(ln_no["moe", c - 2])
            eng.wait_ge(x_mixed, NT)
            nc.gpsimd.memset(small[:, 41:42], 0.0).then_inc(moe_free, 1)
            for i in range(NT - 2, NT):
                scale_ln(ln_no["moe", i])
            own()
            eng.wait_ge(ln_scaled, ln_no["moe", NT - 1] + 1)
            eng.wait_ge(moe_free, 2)
            nc.gpsimd.memset(W2[H - 2 * P:P, :, 2, :], 0.0).then_inc(pool_init, 1)
            eng.wait_ge(pool_init, 2)
            eng.wait_ge(route_done, 1)
            eng.wait_ge(ln_done, 2 * NT)
            eng.wait_ge(zeroed, 16)
            for i in range(NT):
                nc.gpsimd.indirect_dma_start(
                    out=xd_d, out_offset=bass.IndirectOffsetOnAxis(ap=slot_u[:, 0, i:i + 1], axis=0),
                    in_=xn[:, i, :], in_offset=None, bounds_check=E * CAP - 1, oob_is_err=False).then_inc(scattered, 16)
            eng.wait_ge(loaded["tables"], 16)
            for qk, factor in ((0, DH ** -0.5 * Q_SCALE), (1, K_SCALE)):
                mark(ts(ln_w[:, :, qk, :], ln_w[:, :, qk, :], factor, 0.0, ALU.mult, ALU.add))
                mark(ts(ln_b[:, :, qk, :], ln_b[:, :, qk, :], factor, 0.0, ALU.mult, ALU.add))
            own()
            eng.wait_ge(w_split, W_PARTS)
            eng.wait_ge(oe_stored, 16 * E)
            landed(eng, ("xdT", 3))
            for i in range(NT):
                nc.gpsimd.indirect_dma_start(
                    out=og[:, i, :], out_offset=None, in_=oe_d,
                    in_offset=bass.IndirectOffsetOnAxis(ap=slot_u[:, 1, i:i + 1], axis=0),
                    bounds_check=E * CAP - 1, oob_is_err=False).then_inc(gathered[i], 16)

            def rope_tables(i):
                cos, sin = (rope_cs[:, a, i, :].unsqueeze(1).to_broadcast([P, 2, 64]) for a in range(2))
                if i:
                    eng.wait_ge(rope_r, rope_no[i - 1, 3] + 1)
                    eng.wait_ge(rope_i, rope_no[i - 1, 3] + 1)
                    landed(eng, ("eT", i - 1))
                for s, (w, cs) in enumerate(((0, cos), (1, sin), (0, sin), (1, cos))):
                    mark(tt(rt[:, s], ln_w[:, w], cs, ALU.mult))
                t = rtmp.rearrange("p (s qk d) -> p s qk d", s=2, qk=2)
                for half, (c0, c1, op) in enumerate(((cos, sin, ALU.subtract), (sin, cos, ALU.add))):
                    mark(tt(t[:, 0], ln_b[:, 0], c0, ALU.mult))
                    mark(tt(t[:, 1], ln_b[:, 1], c1, ALU.mult))
                    own()
                    ins = tt(rope_E[:, :, half * 64:(half + 1) * 64], t[:, 0], t[:, 1], op)
                    if half:
                        ins.then_inc(tab_ready, 1)
                    else:
                        mark(ins)
                        own()

            def beside_pool(work):
                kind, i, *rest = work
                if kind in ("ln3", "ln4"):
                    scale_ln(ln_no[kind, i])
                    if kind == "ln3" and i:
                        rope_tables(i)
                elif kind == "proj" and rest[0] != "v":
                    r_no = rope_no[i, rest[0]]
                    b = r_no % 2
                    eng.wait_ge(q_stats, r_no + 1)
                    inv_sqrt(q_rs[:, b, :], q_mv[:, b, :, 1], q_tt[:, b, :], 1.0, 1e-6, 4).then_inc(q_rstd, 1)
                elif kind == "rope":
                    r_no = rope_no[i, rest[0]]
                    qk = int(rest[0] == "k")
                    eng.wait_ge(q_norm, r_no + 1)
                    if r_no:
                        eng.wait_ge(rope_i, r_no)
                    table = lambda s: rt[:, s, qk, :].unsqueeze(1).to_broadcast([P, 4, 64])
                    mark(tt(t_i[:, 0], raw_of(r_no)[:, :, 0:64], table(2), ALU.mult))
                    mark(tt(t_i[:, 1], raw_of(r_no)[:, :, 64:128], table(3), ALU.mult))
                    own()
                    if r_no > 4:
                        eng.wait_ge(qk_split, r_no)
                    tt(roped_of(r_no)[:, :, 64:128], t_i[:, 0], t_i[:, 1], ALU.add).then_inc(rope_i, 1)
                elif kind == "h3T":
                    taken(eng, work)
                    tt(h3T[i % 2][:, 1], h3_full, h3T[i % 2][:, 0], ALU.subtract).then_inc(h3_split, 1)
                    if i == 0:
                        rope_tables(0)
                elif kind == "split":
                    r_no, half = rope_no[i, rest[0]], qk_of(work)
                    eng.wait_ge(qk_hi, r_no + 1)
                    tt(half(1), sum_of(r_no), half(0), ALU.subtract).then_inc(qk_split, 1)
                elif kind == "gate":
                    no = 4 * i + rest[0]
                    taken(eng, work)
                    ts(gate[:, no % 2, :], gate[:, no % 2, :], 0.5, 0.5, ALU.mult, ALU.add).then_inc(gate_ready, 1)

            for att, beside in steps:
                for work in beside:
                    beside_pool(work)


def shape_constants():
    k = np.arange(P)
    ident = np.eye(P, dtype=np.float32)
    tri = (k[:, None] <= k[None, :]).astype(np.float32)
    stril = (k[:, None] > k[None, :]).astype(np.float32)
    rank_weight = np.tile(np.arange(E, 0, -1), NT)[None].repeat(P, 0).astype(np.float32)
    base = np.tile(np.arange(E) * CAP, NT)[None].repeat(P, 0).astype(np.float32)
    consts = np.concatenate([ident, tri, stril, rank_weight, base], axis=1)
    inv = np.float32(1.0) / np.float32(1000000.0) ** (np.arange(0, DH, 2, dtype=np.float32) / np.float32(DH))
    freqs = np.outer(np.arange(T, dtype=np.float32), inv.astype(np.float32)).astype(np.float32)
    cs = np.stack([np.cos(freqs), np.sin(freqs)]).astype(np.float32)
    tables = cs.reshape(2, NT, P, 64).transpose(2, 0, 1, 3).reshape(P, -1)
    return np.ascontiguousarray(consts), np.ascontiguousarray(tables)


def kernel(**inputs):
    import numpy as np
    import concourse.bacc as bacc
    from concourse import mybir
    from concourse.bass_utils import run_bass_kernel_spmd as run

    a = {name: np.asarray(value) for name, value in inputs.items()}
    consts, tables = shape_constants()
    cols = lambda t, n: t.reshape(n, P).T
    rows = lambda t: np.broadcast_to(t.reshape(1, -1), (P, t.size))
    even_odd = np.concatenate([np.arange(0, DH, 2), np.arange(1, DH, 2)])
    conv_w = a["L0_attn_conv_w"].reshape(5, P, 4).transpose(1, 0, 2).reshape(P, 20)
    norm = lambda kind: [rows(np.concatenate([a[f"L1_attn_{q}_norm_{kind}"][even_odd[ri * 64:ri * 64 + 64]]
                                              for ri in range(2) for q in "qk"]))]
    vectors = np.concatenate(
        [cols(a["L0_c"].reshape(-1), 2), cols(a["L1_c"].reshape(-1), 2), rows(a["L0_attn_dt_bias"]),
         rows(a["L0_attn_A_log"]), rows(a["L0_attn_D"]), cols(a["L0_attn_norm_w"], 4), conv_w,
         cols(a["L0_attn_conv_b"], 5), np.zeros((P, 3), np.float32)] + norm("w") + norm("b"), axis=1)
    wqkv = a["L1_attn_w_qkv"].reshape(5120 // DH, DH, D)
    perm = np.concatenate([wqkv[0:HQ][:, even_odd], wqkv[HQ:2 * HQ],
                           wqkv[2 * HQ:2 * HQ + HKV][:, even_odd], wqkv[2 * HQ + HKV:]])
    arrays = {
        "consts": consts, "tables": tables, "vectors": vectors, "x": a["L0_attn_u"],
        "W_in": a["L0_attn_W_in"], "W_out": a["L0_attn_W_out"], "Wg": a["L0_ffn_Wg"],
        "W1": a["L0_ffn_W1"], "W3": a["L0_ffn_W3"], "W2": a["L0_ffn_W2"], "sw1": a["L0_ffn_sw1"],
        "sw3": a["L0_ffn_sw3"], "sw2": a["L0_ffn_sw2"], "wmod0": a["L0_wmod"], "wmod1": a["L1_wmod"],
        "wqkv": perm.reshape(5120, D).T, "wo": a["L1_attn_w_o"].T, "wgate": a["L1_ffn_w_gate"],
        "wup": a["L1_ffn_w_up"], "wdown": a["L1_ffn_w_down"],
    }
    arrays = {f"in_{name}": np.ascontiguousarray(t) for name, t in arrays.items()}
    nc = bacc.Bacc("TRN2", target_bir_lowering=False, num_devices=1)
    args = [nc.dram_tensor(name, t.shape, mybir.dt.from_np(t.dtype), kind="ExternalInput").ap()
            for name, t in arrays.items()]
    out = nc.dram_tensor("out", (1, T, D), mybir.dt.float32, kind="ExternalOutput").ap()
    build(nc, *args, out)
    return run(nc, [arrays], core_ids=[0]).results[0]["out"]
```
